# Optimizing a Trainium2 kernel written in Bass

```python
import numpy as np
import jax
import jax.numpy as jnp

def _softmax(x, axis=-1):
    return jax.nn.softmax(x, axis=axis)
def _gelu(x):
    return jax.nn.gelu(x, approximate=True)
def _silu(x):
    return jax.nn.silu(x)
def _sigmoid(x):
    return jax.nn.sigmoid(x)
def _layernorm(x, axis=-1, eps=1e-5):
    m = jnp.mean(x, axis=axis, keepdims=True)
    v = jnp.var(x, axis=axis, keepdims=True)
    return (x - m) / jnp.sqrt(v + eps)
def _scatter_add(tgt, idx, src, axis=0):
    return tgt.at[idx].add(src)
def _segment_sum(src, seg, n):
    return jax.ops.segment_sum(src, seg, n)

kernel_name = 'mk_metaformer_d1_conv_nchw512_42a2f5'

def setup_inputs(seed: int = 0):
    np.random.seed(seed)
    _w = jnp.asarray
    def _rec_inputs():
        import jax
        import jax.numpy as jnp
        _gk = jax.random.key(seed)
        x = 7.22e-05 + 1 * jax.random.normal(jax.random.fold_in(_gk, 1), (16, 512, 32, 32), jnp.float32)
        return x
    x = _rec_inputs()
    def _L0_conv_setup():
        import jax, jax.numpy as jnp
        import numpy as np
        NUM_HEADS = 8
        key = jax.random.key(seed)
        k1, k2, k3 = jax.random.split(key, 3)
        b, c, h, w = (16, 512, 32, 32)
        x = jax.random.normal(k1, (b, c, h, w), dtype=jnp.float32)
        w_qkv = jax.random.normal(k2, (3 * c, c), dtype=jnp.float32) * (1.0 / np.sqrt(c))
        w_proj = jax.random.normal(k3, (c, c), dtype=jnp.float32) * (1.0 / np.sqrt(c))
        b_proj = jnp.zeros((c,), dtype=jnp.float32)
        return {'x': x, 'w_qkv': w_qkv, 'w_proj': w_proj, 'b_proj': b_proj}
    _L0_conv_all = _L0_conv_setup()
    _L0_conv_in = {k: v for k, v in _L0_conv_all.items() if k in ('w_qkv', 'w_proj', 'b_proj', )}
    del _L0_conv_all

    def _L0_ffn_setup():
        import jax, jax.numpy as jnp
        import numpy as np

        def _haar_dwt2(x):
            a = x[:, ::2, ::2]
            b = x[:, ::2, 1::2]
            c = x[:, 1::2, ::2]
            d = x[:, 1::2, 1::2]
            ll = (a + b + c + d) * 0.5
            lh = (a + b - c - d) * 0.5
            hl = (a - b + c - d) * 0.5
            hh = (a - b - c + d) * 0.5
            return (ll, lh, hl, hh)

        def _haar_idwt2(ll, lh, hl, hh):
            a = (ll + lh + hl + hh) * 0.5
            b = (ll + lh - hl - hh) * 0.5
            c = (ll - lh + hl - hh) * 0.5
            d = (ll - lh - hl + hh) * 0.5
            B, H2, W2 = ll.shape
            out = jnp.zeros((B, 2 * H2, 2 * W2), ll.dtype)
            out = out.at[:, ::2, ::2].set(a)
            out = out.at[:, ::2, 1::2].set(b)
            out = out.at[:, 1::2, ::2].set(c)
            out = out.at[:, 1::2, 1::2].set(d)
            return out

        def _interp_linear_last(x, m):
            n = x.shape[-1]
            pos = jnp.linspace(0.0, 1.0, m, dtype=x.dtype) * (n - 1)
            i0 = jnp.clip(jnp.floor(pos).astype(jnp.int32), 0, n - 2)
            w = pos - i0.astype(x.dtype)
            return x[..., i0] * (1.0 - w) + x[..., i0 + 1] * w
        key = jax.random.key(seed)
        k0, k1, k2 = jax.random.split(key, 3)
        b, f, c, hidden = (128, 256, 512, 2048)
        x = jax.random.normal(k0, (b, f, c), dtype=jnp.float32)
        fc1_w = jax.random.normal(k1, (hidden, c), dtype=jnp.float32) * 0.02
        fc1_b = jnp.zeros((hidden,), dtype=jnp.float32)
        fc2_w = jax.random.normal(k2, (c // 2, hidden), dtype=jnp.float32) * 0.02
        fc2_b = jnp.zeros((c // 2,), dtype=jnp.float32)
        return {'x': x, 'fc1_w': fc1_w, 'fc1_b': fc1_b, 'fc2_w': fc2_w, 'fc2_b': fc2_b}
    _L0_ffn_all = _L0_ffn_setup()
    _L0_ffn_in = {k: v for k, v in _L0_ffn_all.items() if k in ('fc1_w', 'fc1_b', 'fc2_w', 'fc2_b', )}
    del _L0_ffn_all

    return {
        "x": x,
        "L0_conv_w_qkv": _L0_conv_in["w_qkv"],
        "L0_conv_w_proj": _L0_conv_in["w_proj"],
        "L0_conv_b_proj": _L0_conv_in["b_proj"],
        "L0_ffn_fc1_w": _L0_ffn_in["fc1_w"],
        "L0_ffn_fc1_b": _L0_ffn_in["fc1_b"],
        "L0_ffn_fc2_w": _L0_ffn_in["fc2_w"],
        "L0_ffn_fc2_b": _L0_ffn_in["fc2_b"],
    }

def reference(x, L0_conv_w_qkv, L0_conv_w_proj, L0_conv_b_proj, L0_ffn_fc1_w, L0_ffn_fc1_b, L0_ffn_fc2_w, L0_ffn_fc2_b):
    import jax
    import jax.numpy as jnp
    def _L0_conv_ref(x, w_qkv, w_proj, b_proj):
        import jax, jax.numpy as jnp
        import numpy as np
        NUM_HEADS = 8
        b, c, h, w = x.shape
        n = h * w
        hd = c // NUM_HEADS
        x_flat = x.reshape(b, c, n)
        qkv = jnp.einsum('dc,bcn->bdn', w_qkv, x_flat)
        q, k, v = jnp.split(qkv, 3, axis=1)
        q = q.reshape(b, NUM_HEADS, hd, n)
        k = k.reshape(b, NUM_HEADS, hd, n)
        v = v.reshape(b, NUM_HEADS, hd, n)
        k = jax.nn.softmax(k, axis=-1)
        q = jax.nn.softmax(q, axis=-2)
        qv = jnp.einsum('bhct,bhdt->bhcd', q, v)
        out = jnp.einsum('bhcd,bhdn->bhcn', qv, k)
        out = out.reshape(b, c, n)
        out = jnp.einsum('dc,bcn->bdn', w_proj, out) + b_proj[None, :, None]
        return out.reshape(b, c, h, w)

    def _L0_ffn_ref(x, fc1_w, fc1_b, fc2_w, fc2_b):
        import jax, jax.numpy as jnp
        import numpy as np

        def _haar_dwt2(x):
            a = x[:, ::2, ::2]
            b = x[:, ::2, 1::2]
            c = x[:, 1::2, ::2]
            d = x[:, 1::2, 1::2]
            ll = (a + b + c + d) * 0.5
            lh = (a + b - c - d) * 0.5
            hl = (a - b + c - d) * 0.5
            hh = (a - b - c + d) * 0.5
            return (ll, lh, hl, hh)

        def _haar_idwt2(ll, lh, hl, hh):
            a = (ll + lh + hl + hh) * 0.5
            b = (ll + lh - hl - hh) * 0.5
            c = (ll - lh + hl - hh) * 0.5
            d = (ll - lh - hl + hh) * 0.5
            B, H2, W2 = ll.shape
            out = jnp.zeros((B, 2 * H2, 2 * W2), ll.dtype)
            out = out.at[:, ::2, ::2].set(a)
            out = out.at[:, ::2, 1::2].set(b)
            out = out.at[:, 1::2, ::2].set(c)
            out = out.at[:, 1::2, 1::2].set(d)
            return out

        def _interp_linear_last(x, m):
            n = x.shape[-1]
            pos = jnp.linspace(0.0, 1.0, m, dtype=x.dtype) * (n - 1)
            i0 = jnp.clip(jnp.floor(pos).astype(jnp.int32), 0, n - 2)
            w = pos - i0.astype(x.dtype)
            return x[..., i0] * (1.0 - w) + x[..., i0 + 1] * w
        b, f, c = x.shape
        ll, lh, hl, hh = _haar_dwt2(x)
        ll_up = _interp_linear_last(ll, c)
        h = jax.nn.gelu(jnp.einsum('bfc,hc->bfh', ll_up, fc1_w) + fc1_b, approximate=False)
        ll_new = jnp.einsum('bfh,oh->bfo', h, fc2_w) + fc2_b
        return _haar_idwt2(ll_new, lh, hl, hh)

    def _gn(v, G=32, eps=1e-5):
        B_, C_, H_, W_ = v.shape
        g = v.reshape(B_, G, C_ // G, H_, W_)
        m = jnp.mean(g, axis=(2, 3, 4), keepdims=True)
        s = jnp.var(g, axis=(2, 3, 4), keepdims=True)
        return ((g - m) / jnp.sqrt(s + eps)).reshape(v.shape)

    def _ln_c(v, eps=1e-6):
        m = jnp.mean(v, axis=1, keepdims=True)
        s = jnp.var(v, axis=1, keepdims=True)
        return (v - m) / jnp.sqrt(s + eps)

    def _ln_t(v, eps=1e-5):
        m = jnp.mean(v, axis=-1, keepdims=True)
        s = jnp.var(v, axis=-1, keepdims=True)
        return (v - m) / jnp.sqrt(s + eps)

    def _to_tokens(v):
        B_, C_, H_, W_ = v.shape
        return v.reshape(B_, C_, H_ * W_).transpose(0, 2, 1)
    def _from_tokens(t, like):
        B_, C_, H_, W_ = like.shape
        return t.transpose(0, 2, 1).reshape(B_, C_, H_, W_)

    x = x + _L0_conv_ref(_ln_c(x), L0_conv_w_qkv, L0_conv_w_proj, L0_conv_b_proj)
    t = _to_tokens(x)
    t = t + _L0_ffn_ref(_ln_t(t), L0_ffn_fc1_w, L0_ffn_fc1_b, L0_ffn_fc2_w, L0_ffn_fc2_b)
    x = _from_tokens(t, x)
    return x


_drawn_inputs = setup_inputs


def setup_inputs(seed=0):
    import zlib

    import numpy as np

    out = dict(_drawn_inputs(seed))
    spreads = {'L0_conv_b_proj': (0.0, 0.67), 'L0_ffn_fc1_b': (0.0, 2.0), 'L0_ffn_fc2_b': (0.0, 1.542)}
    factors = {'L0_conv_w_qkv': 4.435,
     'L0_conv_w_proj': 4.394,
     'L0_ffn_fc1_w': 5.221,
     'L0_ffn_fc2_w': 2.699}
    for name, (base, spread) in spreads.items():
        noise = np.random.default_rng([zlib.crc32(name.encode()), seed]).standard_normal(out[name].shape)
        drawn = base * np.exp(spread * noise) if base else spread * noise
        out[name] = jnp.asarray(drawn.astype(out[name].dtype))
    for name, factor in factors.items():
        out[name] = (out[name] * factor).astype(out[name].dtype)
    return out
```

```python
from contextlib import ExitStack

import concourse.bass as bass
from concourse import mybir

F32 = mybir.dt.float32
F32R = mybir.dt.float32r
F16 = mybir.dt.float16
I32 = mybir.dt.int32
ALU = mybir.AluOpType
ACT = mybir.ActivationFunctionType
AX = mybir.AxisListType
RMAX = bass.bass_isa.ReduceOp.max

P = 128
B = 16
C = 512
J = C // P
N = 1024
H = N // 2
HD = 64
HEADS = C // HD
PAIRS = HEADS // 2
CHUNKS = N // P
HID = 2048
G = HID // P
M2 = C // 2
MT = M2 // P
T2 = N // 2
LN_C_EPS = 1e-6
LN_T_EPS = 1e-5

X_SCALE = 1024.0
E_SCALE = 32768.0
V_SCALE = 2.0 ** -19


MEAN_PE = (4, 6)
VAR_PE = (8, 11)
MEAN_AT = (4, 6)
VAR_AT = (8, 11)


class Count:

    def __init__(self, sem, per, primed=False):
        self.sem, self.per, self.primed = sem, per, primed

    def at(self, b, n):
        return (b + (1 if self.primed else 0)) * self.per + n


def wait(eng, count, b, n):
    eng.wait_ge(count.sem, count.at(b, n))


class Norm:

    def __init__(self, nc, ctx, tag, eps, bank, ones):
        def sb(name, shape, dt=F32):
            return ctx.enter_context(nc.sbuf_tensor(f"{name}_{tag}", shape, dt))

        def cnt(name, per):
            return Count(ctx.enter_context(nc.semaphore(f"{name}_{tag}")), per)

        self.nc, self.eps, self.bank, self.ones = nc, eps, bank, ones
        self.pair_sum = sb("pair_sum", [P, 2, H])
        self.x_sum = sb("x_sum", [P, 2, H])
        self.sq = sb("sq", [P, J, H])
        self.sq_sum = sb("sq_sum", [P, 2, H])
        self.r0 = sb("r0", [P, H])
        self.step = sb("step", [P, H])
        self.m2r = sb("m2r", [P, H])
        self.x_pair = cnt("x_pair", 2)
        self.x_summed = cnt("x_summed", 2)
        self.mean = cnt("mean", 2)
        self.centred = cnt("centred", 2)
        self.squared = cnt("squared", 2)
        self.sq_pair = cnt("sq_pair", 2)
        self.sq_summed = cnt("sq_summed", 2)
        self.var = cnt("var", 2)
        self.logged = cnt("logged", 2)
        self.guessed = cnt("guessed", 2)
        self.guess_sq = cnt("guess_sq", 2)
        self.guess_err = cnt("guess_err", 2)
        self.inv_dev = cnt("inv_dev", 2)

    def pool_sum(self, pool, x, b, h):
        t = slice(h * H, h * H + H)
        if h:
            wait(pool, self.x_summed, b, h)
        elif not (isinstance(b, int) and b == 0):
            wait(pool, self.sq_summed, b - 1, 2)
        self.nc.gpsimd.tensor_tensor(self.pair_sum[:, :, :], x[:, 0:2, t], x[:, 2:4, t],
                                     ALU.add).then_inc(self.x_pair.sem, 1)
        wait(pool, self.x_pair, b, h + 1)
        self.nc.gpsimd.tensor_tensor(self.x_sum[:, h, :], self.pair_sum[:, 0, :], self.pair_sum[:, 1, :],
                                     ALU.add).then_inc(self.x_summed.sem, 1)

    def pe_mean(self, pe, b, h, bank_free=None):
        wait(pe, self.x_summed, b, h + 1)
        if bank_free is not None:
            bank_free(pe, b, h)
        self.nc.tensor.matmul(self.bank[:, :], self.ones[:, :], self.x_sum[:, h, :], start=True,
                              stop=True).then_inc(self.mean.sem, 1)

    def dve_centre(self, dve, x, out, b, h):
        t = slice(h * H, h * H + H)
        wait(dve, self.mean, b, h + 1)
        self.nc.vector.tensor_tensor(out[:, :, t], x[:, :, t],
                                     self.bank[:, :].unsqueeze(1).broadcast_to((P, J, H)),
                                     ALU.subtract).then_inc(self.centred.sem, 1)

    def act_square(self, act, xc, b, h):
        t = slice(h * H, h * H + H)
        wait(act, self.centred, b, h + 1)
        if h:
            wait(act, self.sq_pair, b, h)
        self.nc.scalar.activation(self.sq[:, :, :], xc[:, :, t], ACT.Square).then_inc(self.squared.sem, 1)

    def pool_sq_sum(self, pool, b, h):
        wait(pool, self.squared, b, h + 1)
        if h:
            wait(pool, self.sq_summed, b, h)
        else:
            wait(pool, self.x_summed, b, 2)
        self.nc.gpsimd.tensor_tensor(self.pair_sum[:, :, :], self.sq[:, 0:2, :], self.sq[:, 2:4, :],
                                     ALU.add).then_inc(self.sq_pair.sem, 1)
        wait(pool, self.sq_pair, b, h + 1)
        self.nc.gpsimd.tensor_tensor(self.sq_sum[:, h, :], self.pair_sum[:, 0, :], self.pair_sum[:, 1, :],
                                     ALU.add).then_inc(self.sq_summed.sem, 1)

    def pe_var(self, pe, b, h):
        wait(pe, self.sq_summed, b, h + 1)
        if h:
            wait(pe, self.guess_err, b, h)
        else:
            wait(pe, self.centred, b, 2)
        self.nc.tensor.matmul(self.bank[:, :], self.ones[:, :], self.sq_sum[:, h, :], start=True,
                              stop=True).then_inc(self.var.sem, 1)

    def act_guess(self, act, b, h):
        wait(act, self.var, b, h + 1)
        if h:
            wait(act, self.inv_dev, b, h)
        self.nc.scalar.activation(self.r0[:, :], self.bank[:, :], ACT.Ln,
                                  bias=self.eps_col).then_inc(self.logged.sem, 1)
        wait(act, self.logged, b, h + 1)
        self.nc.scalar.activation(self.r0[:, :], self.r0[:, :], ACT.Exp,
                                  scale=-0.5).then_inc(self.guessed.sem, 1)

    def dve_newton(self, dve, b, h):
        nc = self.nc
        wait(dve, self.guessed, b, h + 1)
        nc.vector.tensor_tensor(self.step[:, :], self.r0[:, :], self.r0[:, :],
                                ALU.mult).then_inc(self.guess_sq.sem, 1)
        wait(dve, self.guess_sq, b, h + 1)
        nc.vector.scalar_tensor_tensor(self.step[:, :], self.bank[:, :], self.eps, self.step[:, :],
                                       ALU.add, ALU.mult).then_inc(self.guess_err.sem, 1)
        wait(dve, self.guess_err, b, h + 1)
        nc.vector.scalar_tensor_tensor(self.m2r[:, :], self.step[:, :], 3.0, self.r0[:, :],
                                       ALU.subtract, ALU.mult).then_inc(self.inv_dev.sem, 1)


def split3(nc, out, a_hi, a_lo, b_hi, b_lo, start, stop, skip=False):
    nc.tensor.matmul(out, a_hi, b_hi, start=start, stop=False, skip_group_check=skip)
    nc.tensor.matmul(out, a_hi, b_lo, start=False, stop=False, skip_group_check=skip)
    return nc.tensor.matmul(out, a_lo, b_hi, start=False, stop=stop, skip_group_check=skip)


def attention(nc, x_dram, wqkv_dram, wproj_dram, bproj_dram, x1_dram):
    ctx = ExitStack()
    with ctx:
        def sb(name, shape, dt=F32):
            return ctx.enter_context(nc.sbuf_tensor(name, shape, dt))

        def sem(name):
            return ctx.enter_context(nc.semaphore(name))

        def cnt(name, per, primed=False):
            return Count(sem(name), per, primed)

        wq_hi = sb("wq_hi", [P, J, 3 * C], F16)
        wq_lo = sb("wq_lo", [P, J, 3 * C], F16)
        wp_hi = sb("wp_hi", [P, PAIRS, C], F32R)
        wp_lo = sb("wp_lo", [P, PAIRS, C], F32R)
        xb = sb("xb", [P, 2, J, N])
        stage = xb[:, :, :, :].rearrange("p a j n -> p (a j n)")
        wq_st = stage[:, 0:J * 3 * C]
        wp_st = stage[:, J * 3 * C:J * 3 * C + PAIRS * C]
        xc = sb("xc", [P, J, N])
        xn_hi = sb("xn_hi", [P, J, N], F16)
        xn_lo = sb("xn_lo", [P, J, N], F16)
        e_tmp = sb("e_tmp", [P, 2, N])
        ek_hi = sb("ek_hi", [P, PAIRS, N], F32R)
        ek_lo = sb("ek_lo", [P, PAIRS, N], F32R)
        eq = sb("eq", [P, 2, C])
        vn = sb("vn", [P, 2, C])
        eq_hi = sb("eq_hi", [P, 2, C], F16)
        eq_lo = sb("eq_lo", [P, 2, C], F16)
        vn_hi = sb("vn_hi", [P, 2, C], F16)
        vn_lo = sb("vn_lo", [P, 2, C], F16)
        qv_hi = sb("qv_hi", [P, PAIRS, P], F32R)
        qv_lo = sb("qv_lo", [P, PAIRS, P], F32R)
        mt_hi = sb("mt_hi", [P, PAIRS, C], F32R)
        mt_lo = sb("mt_lo", [P, PAIRS, C], F32R)
        ones = sb("ones", [P, P])
        bproj = sb("bproj", [P, J])
        small = sb("small", [P, 8])
        eps_col = sb("eps_col", [P, 1])
        row_max, all_max, exp_bits = small[:, 0:1], small[:, 1:2], small[:, 2:3]
        w_scale, un_scale, m_scale = small[:, 3:4], small[:, 4:5], small[:, 5:6]
        k_max = sb("k_max", [P, PAIRS])
        k_bias = sb("k_bias", [P, PAIRS])
        k_sum = sb("k_sum", [P, PAIRS])
        k_inv = sb("k_inv", [P, PAIRS])
        k_gain = sb("k_gain", [P, PAIRS])
        q_max = sb("q_max", [P, 2, HEADS])
        q_sum = sb("q_sum", [P, 2, HEADS])
        q_inv = sb("q_inv", [P, 2, HEADS])

        ring = [ctx.enter_context(nc.psum_tensor(f"ring{i}", [P, 2, H], F32)) for i in range(3)]
        qv_bank = ctx.enter_context(nc.psum_tensor("qv_bank", [P, PAIRS, P], F32))
        nbank = ctx.enter_context(nc.psum_tensor("norm_bank", [P, H], F32))
        norm = Norm(nc, ctx, "a", LN_C_EPS, nbank, ones)
        norm.eps_col = eps_col[:, 0:1]

        w_in = sem("w_in")
        prep = sem("prep")
        wq_hi_done = sem("wq_hi_done")
        w_ready = sem("w_ready")
        consts = sem("consts")
        xl = cnt("x_loaded", 16)
        x1_stored = cnt("x1_stored", 32)
        xs = cnt("x_scaled", 2)
        xhi = cnt("xn_hi_ready", 2)
        xlo = cnt("xn_lo_ready", 2)
        k_full = cnt("k_full", PAIRS)
        k_maxed = cnt("k_maxed", PAIRS)
        k_biased = cnt("k_biased", PAIRS)
        k_exp = cnt("k_exp", PAIRS)
        ek_hi_r = cnt("ek_hi_ready", PAIRS)
        ek_lo_r = cnt("ek_lo_ready", PAIRS, True)
        q_full = cnt("q_full", CHUNKS)
        v_full = cnt("v_full", CHUNKS)
        q_maxed = cnt("q_maxed", CHUNKS)
        q_shift = cnt("q_shifted", CHUNKS)
        q_exp = cnt("q_exp", CHUNKS)
        q_summed = cnt("q_summed", CHUNKS)
        q_inved = cnt("q_inverted", CHUNKS)
        v_norm = cnt("v_normed", CHUNKS)
        eq_hi_r = cnt("eq_hi_ready", CHUNKS)
        eq_lo_r = cnt("eq_lo_ready", CHUNKS)
        vn_hi_r = cnt("vn_hi_ready", CHUNKS)
        vn_lo_r = cnt("vn_lo_ready", CHUNKS, True)
        qv_used = cnt("qv_used", CHUNKS, True)
        qv_hi_r = cnt("qv_hi_ready", 2)
        qv_lo_r = cnt("qv_lo_ready", 2, True)
        k_inved = cnt("k_inverted", 1)
        k_gained = cnt("k_gain_ready", 1)
        m_full = cnt("m_full", PAIRS)
        mt_hi_r = cnt("mt_hi_ready", PAIRS)
        mt_lo_r = cnt("mt_lo_ready", PAIRS)
        o_full = cnt("o_full", J, True)
        x1_r = cnt("x1_ready", J, True)

        block = ctx.enter_context(nc.Block())

        def batches(eng, body):
            with eng.Fori(0, B // 2 - 1) as i:
                for par in range(2):
                    body(i * 2 + par, par, False)
            for par in range(2):
                body(B - 2 + par, par, True)

        @block.sync
        def _(sp):
            sp.dma_start(wq_st, wqkv_dram).then_inc(w_in, 16)
            sp.dma_start(wp_st, wproj_dram).then_inc(w_in, 16)
            sp.dma_start(bproj[:, :], bproj_dram).then_inc(w_in, 16)
            sp.wait_ge(w_ready, 4)
            for b in range(2):
                if b:
                    wait(sp, xl, b - 1, 16)
                sp.dma_start(xb[:, b, :, :], x_dram[b]).then_inc(xl.sem, 16)

            def body(b, par, last):
                for half in range(2):
                    j = slice(2 * half, 2 * half + 2)
                    wait(sp, x1_r, b, 2 * half + 2)
                    sp.dma_start(x1_dram[b][:, j, :], xb[:, par, j, :]).then_inc(x1_stored.sem, 16)
                wait(sp, x1_stored, b, 32)
                if not last:
                    sp.dma_start(xb[:, par, :, :], x_dram[b + 2]).then_inc(xl.sem, 16)

            batches(sp, body)

        @block.gpsimd
        def _(pool):
            nc.gpsimd.memset(ones[:, :], 1.0 / C).then_inc(consts, 1)
            nc.gpsimd.memset(eps_col[:, :], LN_C_EPS).then_inc(consts, 1)
            nc.gpsimd.memset(qv_hi[:, :, :].bitcast(F32), 0.0).then_inc(consts, 1)
            nc.gpsimd.memset(qv_lo[:, :, :].bitcast(F32), 0.0).then_inc(consts, 1)
            pool.sem_inc(ek_lo_r.sem, PAIRS)
            pool.sem_inc(vn_lo_r.sem, CHUNKS)
            pool.wait_ge(prep, 1)
            nc.gpsimd.partition_all_reduce(all_max, row_max, P, RMAX).then_inc(prep, 1)

            def norm_sums(b, par):
                wait(pool, xl, b, 16)
                for h in range(2):
                    norm.pool_sum(pool, xb[:, par, :, :], b, h)

            def xn_low(b, h):
                t = slice(h * H, h * H + H)
                wait(pool, xhi, b, h + 1)
                nc.gpsimd.tensor_tensor(xn_lo[:, :, t], xc[:, :, t], xn_hi[:, :, t],
                                        ALU.subtract).then_inc(xlo.sem, 1)

            def k_low(b, j):
                wait(pool, ek_hi_r, b, j + 1)
                nc.gpsimd.tensor_tensor(ek_lo[:, j, :], e_tmp[:, j % 2, :], ek_hi[:, j, :].bitcast(F32),
                                        ALU.subtract).then_inc(ek_lo_r.sem, 1)

            def v_low(b, t):
                wait(pool, vn_hi_r, b, t + 1)
                nc.gpsimd.tensor_tensor(vn_lo[:, t % 2, :], vn[:, t % 2, :], vn_hi[:, t % 2, :],
                                        ALU.subtract).then_inc(vn_lo_r.sem, 1)

            norm_sums(0, 0)
            for h in range(2):
                norm.pool_sq_sum(pool, 0, h)
            for h in range(2):
                xn_low(0, h)

            def body(b, par, last):
                more = not (last and par)
                k_low(b, 0)
                k_low(b, 1)
                if more:
                    norm_sums(b + 1, 1 - par)
                for t in range(1, CHUNKS):
                    v_low(b, t - 1)
                    if more and t in (4, 5):
                        norm.pool_sq_sum(pool, b + 1, t - 4)
                v_low(b, CHUNKS - 1)
                k_low(b, 2)
                k_low(b, 3)
                if more:
                    for h in range(2):
                        xn_low(b + 1, h)

            batches(pool, body)

        @block.scalar
        def _(act):
            act.wait_ge(consts, 4)
            act.wait_ge(prep, 5)
            nc.scalar.activation(wq_hi[:, :, :], wq_st.rearrange("p (j n) -> p j n", j=J), ACT.Copy,
                                 scale=w_scale).then_inc(wq_hi_done, 1)
            nc.scalar.activation(wp_hi[:, :, :], wp_st.rearrange("p (j n) -> p j n", j=PAIRS),
                                 ACT.Copy).then_inc(wq_hi_done, 1)

            def xn_high(b, h, free):
                t = slice(h * H, h * H + H)
                wait(act, xs, b, h + 1)
                if free is not None:
                    wait(act, k_full, free, PAIRS)
                nc.scalar.activation(xn_hi[:, :, t], xc[:, :, t], ACT.Copy).then_inc(xhi.sem, 1)

            def k_tile(b, j, s):
                wait(act, k_biased, b, j + 1)
                if j < 2:
                    wait(act, ek_lo_r, b - 1, j + 3)
                else:
                    wait(act, ek_lo_r, b, j - 1)
                nc.scalar.activation(e_tmp[:, j % 2, :], ring[s % 3][:, :, :].rearrange("p a n -> p (a n)"),
                                     ACT.Exp, bias=k_bias[:, j:j + 1], scale=un_scale,
                                     accum_out=k_sum[:, j:j + 1]).then_inc(k_exp.sem, 1)
                wait(act, k_exp, b, j + 1)
                wait(act, o_full, b - 1, J)
                nc.scalar.activation(ek_hi[:, j, :], e_tmp[:, j % 2, :], ACT.Copy).then_inc(ek_hi_r.sem, 1)

            def q_high(b, t):
                wait(act, q_shift, b, t + 1)
                nc.scalar.activation(eq[:, t % 2, :], eq[:, t % 2, :], ACT.Exp,
                                     scale=un_scale).then_inc(q_exp.sem, 1)
                wait(act, q_exp, b, t + 1)
                if t < 2:
                    wait(act, qv_used, b - 1, t + 7)
                else:
                    wait(act, qv_used, b, t - 1)
                nc.scalar.activation(eq_hi[:, t % 2, :], eq[:, t % 2, :], ACT.Copy,
                                     scale=E_SCALE).then_inc(eq_hi_r.sem, 1)

            def v_high(b, t):
                wait(act, v_norm, b, t + 1)
                nc.scalar.activation(vn_hi[:, t % 2, :], vn[:, t % 2, :], ACT.Copy).then_inc(vn_hi_r.sem, 1)

            for h in range(2):
                norm.act_square(act, xc, 0, h)
            for h in range(2):
                norm.act_guess(act, 0, h)
            for h in range(2):
                xn_high(0, h, None)

            def body(b, par, last):
                more = not (last and par)
                k_tile(b, 0, 0)
                k_tile(b, 1, 1)
                for t in range(CHUNKS):
                    if more and t in (6, 7):
                        norm.act_guess(act, b + 1, t - 6)
                    q_high(b, t)
                    if t:
                        v_high(b, t - 1)
                    if more and t in (3, 4):
                        norm.act_square(act, xc, b + 1, t - 3)
                v_high(b, CHUNKS - 1)
                k_tile(b, 2, 10)
                wait(act, qv_used, b, CHUNKS)
                for d in range(2):
                    s = slice(d * HD, d * HD + HD)
                    nc.scalar.activation(qv_hi[s, :, s], qv_bank[s, :, s], ACT.Copy).then_inc(qv_hi_r.sem, 1)
                k_tile(b, 3, 11)
                for p in range(PAIRS):
                    wait(act, m_full, b, p + 1)
                    if p == 0:
                        wait(act, k_gained, b, 1)
                    nc.scalar.activation(mt_hi[:, p, :], ring[(12 + p // 2) % 3][:, p % 2, :], ACT.Copy,
                                         scale=k_gain[:, p:p + 1]).then_inc(mt_hi_r.sem, 1)
                if more:
                    for h in range(2):
                        xn_high(b + 1, h, b)

            batches(act, body)

        @block.vector
        def _(dve):
            dve.wait_ge(w_in, 48)
            nc.vector.tensor_reduce(row_max, wq_st, AX.X, ALU.max, apply_absolute_value=True).then_inc(prep, 1)
            dve.wait_ge(prep, 2)
            nc.vector.tensor_scalar_max(exp_bits, all_max, 1e-30).then_inc(prep, 1)
            dve.wait_ge(prep, 3)
            nc.vector.tensor_scalar(exp_bits.bitcast(I32), exp_bits.bitcast(I32), 0x7F800000, None,
                                    ALU.bitwise_and).then_inc(prep, 1)
            dve.wait_ge(prep, 4)
            nc.vector.tensor_scalar(un_scale.bitcast(I32), exp_bits.bitcast(I32), 1.0, float(-24 * 2 ** 23),
                                    ALU.mult, ALU.add)
            nc.vector.tensor_scalar(m_scale.bitcast(I32), exp_bits.bitcast(I32), 1.0, float(-20 * 2 ** 23),
                                    ALU.mult, ALU.add)
            nc.vector.tensor_scalar(w_scale.bitcast(I32), exp_bits.bitcast(I32), -1.0, float(268 * 2 ** 23),
                                    ALU.mult, ALU.add).then_inc(prep, 1)
            dve.wait_ge(prep, 5)
            dve.sem_inc(x1_r.sem, J)
            dve.sem_inc(qv_lo_r.sem, 2)
            dve.wait_ge(wq_hi_done, 1)
            nc.vector.scalar_tensor_tensor(wq_lo[:, :, :].rearrange("p j n -> p (j n)"), wq_st, w_scale,
                                           wq_hi[:, :, :].rearrange("p j n -> p (j n)"), ALU.mult,
                                           ALU.subtract).then_inc(w_ready, 2)
            dve.wait_ge(wq_hi_done, 2)
            nc.vector.tensor_tensor(wp_lo[:, :, :].rearrange("p j n -> p (j n)"), wp_st,
                                    wp_hi[:, :, :].rearrange("p j n -> p (j n)").bitcast(F32),
                                    ALU.subtract).then_inc(w_ready, 2)

            def x_scale(b, h):
                t = slice(h * H, h * H + H)
                wait(dve, norm.inv_dev, b, h + 1)
                wait(dve, norm.squared, b, h + 1)
                nc.vector.scalar_tensor_tensor(
                    xc[:, :, t], xc[:, :, t], -0.5 * X_SCALE,
                    norm.m2r[:, :].unsqueeze(1).broadcast_to((P, J, H)), ALU.mult, ALU.mult).then_inc(xs.sem, 1)

            def centre(b, par, h):
                if h == 0:
                    wait(dve, xl, b, 16)
                dve_free = b
                norm.dve_centre(dve, xb[:, par, :, :], xc, dve_free, h)

            def k_tile(b, j, s):
                wait(dve, k_full, b, j + 1)
                nc.vector.reduce_max(k_max[:, j:j + 1], ring[s % 3][:, :, :].rearrange("p a n -> p (a n)"),
                                     AX.X).then_inc(k_maxed.sem, 1)
                wait(dve, k_maxed, b, j + 1)
                nc.vector.tensor_scalar(k_bias[:, j:j + 1], k_max[:, j:j + 1], un_scale, -1.0, ALU.mult,
                                        ALU.mult).then_inc(k_biased.sem, 1)

            def heads(ap):
                return ap.rearrange("p (h d) -> p h d", h=HEADS)

            def spread(ap):
                return ap.unsqueeze(2).broadcast_to((P, HEADS, HD))

            def q_shift_chunk(b, t):
                bank = ring[(t + 2) % 3][:, 0, :]
                wait(dve, q_full, b, t + 1)
                nc.vector.reduce_max(q_max[:, t % 2, :], heads(bank), AX.X).then_inc(q_maxed.sem, 1)
                wait(dve, q_maxed, b, t + 1)
                if t >= 2:
                    wait(dve, eq_hi_r, b, t - 1)
                nc.vector.tensor_tensor(heads(eq[:, t % 2, :]), heads(bank), spread(q_max[:, t % 2, :]),
                                        ALU.subtract).then_inc(q_shift.sem, 1)

            def v_chunk(b, t):
                bank = ring[(t + 2) % 3][:, 1, :]
                wait(dve, q_exp, b, t + 1)
                nc.vector.reduce_sum(q_sum[:, t % 2, :], heads(eq[:, t % 2, :]), AX.X).then_inc(q_summed.sem, 1)
                wait(dve, q_summed, b, t + 1)
                nc.vector.reciprocal(q_inv[:, t % 2, :], q_sum[:, t % 2, :]).then_inc(q_inved.sem, 1)
                wait(dve, q_inved, b, t + 1)
                wait(dve, v_full, b, t + 1)
                if t >= 2:
                    wait(dve, vn_lo_r, b, t - 1)
                else:
                    wait(dve, vn_lo_r, b - 1, t + 7)
                nc.vector.scalar_tensor_tensor(heads(vn[:, t % 2, :]), heads(bank), V_SCALE,
                                               spread(q_inv[:, t % 2, :]), ALU.mult,
                                               ALU.mult).then_inc(v_norm.sem, 1)

            def q_low(b, t):
                wait(dve, eq_hi_r, b, t + 1)
                nc.vector.scalar_tensor_tensor(eq_lo[:, t % 2, :], eq[:, t % 2, :], E_SCALE,
                                               eq_hi[:, t % 2, :], ALU.mult,
                                               ALU.subtract).then_inc(eq_lo_r.sem, 1)

            for h in range(2):
                centre(0, 0, h)
            for h in range(2):
                norm.dve_newton(dve, 0, h)
                x_scale(0, h)

            def body(b, par, last):
                more = not (last and par)
                k_tile(b, 0, 0)
                k_tile(b, 1, 1)
                for t in range(CHUNKS):
                    if more and t in (3, 4):
                        if t == 3:
                            wait(dve, xlo, b, 2)
                        centre(b + 1, 1 - par, t - 3)
                    if more and t in (6, 7):
                        norm.dve_newton(dve, b + 1, t - 6)
                        x_scale(b + 1, t - 6)
                    q_shift_chunk(b, t)
                    if t:
                        v_chunk(b, t - 1)
                        q_low(b, t - 1)
                v_chunk(b, CHUNKS - 1)
                q_low(b, CHUNKS - 1)
                k_tile(b, 2, 10)
                for d in range(2):
                    s = slice(d * HD, d * HD + HD)
                    wait(dve, qv_hi_r, b, 2)
                    nc.vector.tensor_tensor(qv_lo[s, :, s], qv_bank[s, :, s], qv_hi[s, :, s].bitcast(F32),
                                            ALU.subtract).then_inc(qv_lo_r.sem, 1)
                k_tile(b, 3, 11)
                wait(dve, k_exp, b, PAIRS)
                nc.vector.reciprocal(k_inv[:, :], k_sum[:, :]).then_inc(k_inved.sem, 1)
                wait(dve, k_inved, b, 1)
                nc.vector.tensor_scalar(k_gain[:, :], k_inv[:, :], m_scale, None,
                                        ALU.mult).then_inc(k_gained.sem, 1)
                wait(dve, k_gained, b, 1)
                for p in range(PAIRS):
                    wait(dve, mt_hi_r, b, p + 1)
                    nc.vector.scalar_tensor_tensor(mt_lo[:, p, :], ring[(12 + p // 2) % 3][:, p % 2, :],
                                                   k_gain[:, p:p + 1], mt_hi[:, p, :].bitcast(F32),
                                                   ALU.mult, ALU.subtract).then_inc(mt_lo_r.sem, 1)
                for j in range(J):
                    wait(dve, o_full, b, j + 1)
                    nc.vector.scalar_tensor_tensor(
                        xb[:, par, j, :], ring[(14 + j) % 3][:, :, :].rearrange("p a n -> p (a n)"),
                        bproj[:, j:j + 1], xb[:, par, j, :], ALU.add, ALU.add).then_inc(x1_r.sem, 1)

            batches(dve, body)

        @block.tensor
        def _(pe):
            pe.sem_inc(o_full.sem, J)
            pe.sem_inc(qv_used.sem, CHUNKS)
            pe.wait_ge(consts, 4)
            pe.wait_ge(w_ready, 4)

            def k_half(b, j, s, h):
                t = slice(h * H, h * H + H)
                w = slice(C + j * P, C + j * P + P)
                for c in range(J):
                    last = split3(nc, ring[s % 3][:, h, :], wq_hi[:, c, w], wq_lo[:, c, w], xn_hi[:, c, t],
                                  xn_lo[:, c, t], c == 0, c == J - 1)
                return last

            def chunk(b, t):
                ts = slice(t * P, t * P + P)
                for part, count in ((0, q_full), (1, v_full)):
                    w = slice(part * 2 * C, part * 2 * C + C)
                    for c in range(J):
                        last = split3(nc, ring[(t + 2) % 3][:, part, :], xn_hi[:, c, ts], xn_lo[:, c, ts],
                                      wq_hi[:, c, w], wq_lo[:, c, w], c == 0, c == J - 1)
                    last.then_inc(count.sem, 1)

            def qv_chunk(b, t):
                wait(pe, eq_lo_r, b, t + 1)
                wait(pe, vn_lo_r, b, t + 1)
                if t == 0:
                    wait(pe, qv_lo_r, b - 1, 2)
                i = t % 2
                for p in range(PAIRS):
                    s = slice(p * P, p * P + P)
                    last = split3(nc, qv_bank[:, p, :], eq_hi[:, i, s], eq_lo[:, i, s], vn_hi[:, i, s],
                                  vn_lo[:, i, s], t == 0 and p == 0, t == CHUNKS - 1, True)
                last.then_inc(qv_used.sem, 1)

            for h in range(2):
                norm.pe_mean(pe, 0, h, lambda e, b, h: wait(e, norm.centred, b, h) if h else None)
            for h in range(2):
                norm.pe_var(pe, 0, h)

            def mean_bank_free(e, b, h):
                if h:
                    wait(e, norm.centred, b, h)
                else:
                    wait(e, norm.guess_err, b - 1, 2)

            def body(b, par, last):
                more = not (last and par)
                for h in range(2):
                    wait(pe, xhi, b, h + 1)
                    wait(pe, xlo, b, h + 1)
                wait(pe, x1_r, b - 1, 2)
                for h in range(2):
                    k = k_half(b, 0, 0, h)
                k.then_inc(k_full.sem, 1)
                wait(pe, x1_r, b - 1, 3)
                for h in range(2):
                    k = k_half(b, 1, 1, h)
                k.then_inc(k_full.sem, 1)
                for t in range(CHUNKS):
                    if t == 0:
                        wait(pe, x1_r, b - 1, 4)
                    elif t < 3:
                        wait(pe, k_exp, b, t)
                    else:
                        wait(pe, v_norm, b, t - 2)
                    chunk(b, t)
                    if t >= 2:
                        qv_chunk(b, t - 2)
                    if more and t in (2, 3):
                        norm.pe_mean(pe, b + 1, t - 2, mean_bank_free)
                    if more and t in (5, 6):
                        norm.pe_var(pe, b + 1, t - 5)
                wait(pe, v_norm, b, 6)
                for h in range(2):
                    k = k_half(b, 2, 10, h)
                k.then_inc(k_full.sem, 1)
                qv_chunk(b, 6)
                wait(pe, v_norm, b, 7)
                k_half(b, 3, 11, 0)
                qv_chunk(b, 7)
                k_half(b, 3, 11, 1).then_inc(k_full.sem, 1)
                wait(pe, qv_lo_r, b, 2)
                for p in range(PAIRS):
                    if p == 0:
                        wait(pe, v_norm, b, 8)
                    if p == 2:
                        wait(pe, k_exp, b, 3)
                    split3(nc, ring[(12 + p // 2) % 3][:, p % 2, :], qv_hi[:, p, :], qv_lo[:, p, :],
                           wp_hi[:, p, :], wp_lo[:, p, :], True, True).then_inc(m_full.sem, 1)
                for j in range(J):
                    if j == 0:
                        wait(pe, k_exp, b, 4)
                    elif j == 3:
                        wait(pe, x1_r, b, 1)
                    js = slice(j * P, j * P + P)
                    for p in range(PAIRS):
                        if j == 0:
                            wait(pe, mt_lo_r, b, p + 1)
                            wait(pe, ek_lo_r, b, p + 1)
                        for h in range(2):
                            t = slice(h * H, h * H + H)
                            last = split3(nc, ring[(14 + j) % 3][:, h, :], mt_hi[:, p, js], mt_lo[:, p, js],
                                          ek_hi[:, p, t], ek_lo[:, p, t], p == 0, p == PAIRS - 1)
                    last.then_inc(o_full.sem, 1)

            batches(pe, body)


def feed_forward(nc, x1_dram, fc1t_dram, fc1b_dram, interp_dram, fc2t_dram, fc2b_dram, out_dram):
    ctx = ExitStack()
    with ctx:
        def sb(name, shape, dt=F32):
            return ctx.enter_context(nc.sbuf_tensor(name, shape, dt))

        def sem(name):
            return ctx.enter_context(nc.semaphore(name))

        def cnt(name, per, primed=False):
            return Count(sem(name), per, primed)

        LAG = 3
        w1_hi = sb("w1_hi", [P, MT, HID], F32R)
        w1_lo = sb("w1_lo", [P, MT, HID], F32R)
        w2_hi = sb("w2_hi", [P, G, M2], F32R)
        w2_lo = sb("w2_lo", [P, G, M2], F32R)
        xb = sb("fx", [P, J, N])
        zb = sb("zb", [P, 2, J, N])
        w1_st = zb[:, :, :, :].rearrange("p a j n -> p (a j n)").rearrange("p (j n) -> p j n", j=J)
        w2_st = xb[:, :, :].rearrange("p j n -> p (j n)").rearrange("p (g m) -> p g m", g=G)
        ones = sb("f_ones", [P, P])
        eps_col = sb("f_eps_col", [P, 1])
        fc1b = sb("fc1b", [P, G])
        fc2b = sb("fc2b", [P, MT])
        mean = sb("mean_row", [P, 2, N])
        gain = sb("gain", [P, N])
        pairc = sb("pairc", [P, MT, H])
        quad = sb("quad", [P, 2, MT, T2])
        ll_hi = sb("ll_hi", [P, MT, T2], F32R)
        ll_lo = sb("ll_lo", [P, MT, T2], F32R)
        ht = sb("ht", [P, 2, T2])
        h_hi = sb("h_hi", [P, 4, T2], F32R)
        h_lo = sb("h_lo", [P, 4, T2], F32R)
        change = sb("change", [P, MT, T2])
        add = sb("add", [P, MT, N])
        interp = add[:, 0, :].rearrange("p (j m) -> p j m", j=J)

        hbank = [ctx.enter_context(nc.psum_tensor(f"hbank{i}", [P, T2], F32)) for i in range(3)]
        obank = ctx.enter_context(nc.psum_tensor("obank", [P, 2, MT, T2], F32))
        nbank = ctx.enter_context(nc.psum_tensor("f_norm_bank", [P, H], F32))
        norm = Norm(nc, ctx, "b", LN_T_EPS, nbank, ones)
        norm.eps_col = eps_col[:, 0:1]

        w_in = sem("f_w_in")
        consts = sem("f_consts")
        w1_full = sem("w1_full")
        w1_hi_r = sem("w1_hi_ready")
        w1_lo_r = sem("w1_lo_ready")
        w2_hi_r = sem("w2_hi_ready")
        w2_lo_r = sem("w2_lo_ready")
        xl = cnt("f_x_loaded", 16)
        meaned = cnt("mean_kept", 2)
        paired = cnt("channel_pairs", 2)
        pair_normed = cnt("pairs_normed", 2)
        quaded = cnt("quads", 2)
        ll_hi_r = cnt("ll_hi_ready", 1)
        ll_lo_r = cnt("ll_lo_ready", 1)
        gained = cnt("gain_ready", 2)
        scaled = cnt("x_gained", 4)
        h_full = cnt("h_full", G)
        h_act = cnt("h_gelu", G)
        h_hi_r = cnt("h_hi_ready", G)
        h_lo_r = cnt("h_lo_ready", G, True)
        h_used = cnt("h_used", G, True)
        changed = cnt("change_raw", MT)
        halved = cnt("change_ready", MT)
        added = cnt("add_ready", MT)
        z_r = cnt("z_ready", J)
        z_stored = [cnt(f"z_stored{par}", 16) for par in range(2)]

        block = ctx.enter_context(nc.Block())

        def batches(eng, body):
            for par in range(2):
                body(par, par, False, par == 0)
            with eng.Fori(1, B // 2 - 1) as i:
                for par in range(2):
                    body(i * 2 + par, par, False, False)
            for par in range(2):
                body(B - 2 + par, par, True, False)

        @block.sync
        def _(sp):
            sp.dma_start(w1_st, fc1t_dram).then_inc(w_in, 16)
            sp.dma_start(interp[:, :, :], interp_dram).then_inc(w_in, 16)
            sp.dma_start(w2_st, fc2t_dram).then_inc(w_in, 16)
            sp.dma_start(fc1b[:, :], fc1b_dram).then_inc(w_in, 16)
            sp.dma_start(fc2b[:, :], fc2b_dram).then_inc(w_in, 16)
            sp.wait_ge(w2_lo_r, 1)
            sp.dma_start(xb[:, :, :], x1_dram[0]).then_inc(xl.sem, 16)

            def store(b, par):
                for half in range(2):
                    j = slice(2 * half, 2 * half + 2)
                    wait(sp, z_r, b, 2 * half + 2)
                    sp.dma_start(out_dram[b][:, j, :], zb[:, par, j, :]).then_inc(z_stored[par].sem, 16)

            def body(b, par, last, first):
                if not (last and par):
                    wait(sp, scaled, b, J)
                    sp.dma_start(xb[:, :, :], x1_dram[b + 1]).then_inc(xl.sem, 16)
                if not first:
                    store(b - 1, 1 - par)
                if last and par:
                    store(b, par)
                    for k in range(2):
                        wait(sp, z_stored[k], b - par, 32)

            batches(sp, body)

        @block.gpsimd
        def _(pool):
            nc.gpsimd.memset(ones[:, :], 1.0 / C).then_inc(consts, 1)
            nc.gpsimd.memset(eps_col[:, :], LN_T_EPS).then_inc(consts, 1)

            def sums(b, par):
                wait(pool, xl, b, 16)
                for h in range(2):
                    norm.pool_sum(pool, xb, b, h)

            def pair(b, par, h):
                t = slice(h * H, h * H + H)
                wait(pool, norm.centred, b, h + 1)
                if h:
                    wait(pool, quaded, b, h)
                nc.gpsimd.tensor_tensor(pairc[:, :, :], xb[:, 0:4:2, t], xb[:, 1:4:2, t],
                                        ALU.add).then_inc(paired.sem, 1)

            def gains(b, par, j):
                wait(pool, gained, b, 2)
                if not (isinstance(b, int) and b < 2):
                    wait(pool, z_stored[par], b - par - 2, 32)
                nc.gpsimd.tensor_tensor(zb[:, par, j, :], xb[:, j, :], gain[:, :],
                                        ALU.mult).then_inc(scaled.sem, 1)

            def pre(b, par):
                sums(b, par)
                for h in range(2):
                    norm.pool_sq_sum(pool, b, h)
                    pair(b, par, h)
                for j in range(J):
                    gains(b, par, j)

            pool.wait_ge(w1_full, MT * 4)
            pre(0, 0)

            def body(b, par, last, first):
                if not (last and par):
                    pre(b + 1, 1 - par)

            batches(pool, body)

        @block.scalar
        def _(act):
            act.wait_ge(consts, 2)
            act.wait_ge(w_in, 80)
            nc.scalar.activation(w2_hi[:, :, :], w2_st, ACT.Copy).then_inc(w2_hi_r, 1)
            for i in range(MT * 4):
                m, n = i // 4, i % 4
                act.wait_ge(w1_full, i + 1)
                nc.scalar.activation(w1_hi[:, m, n * H:n * H + H], hbank[i % 3][:, :],
                                     ACT.Copy).then_inc(w1_hi_r, 1)

            def keep_mean(b, par, h):
                wait(act, norm.centred, b, h + 1)
                nc.scalar.activation(mean[:, par, h * H:h * H + H], nbank[:, :], ACT.Copy).then_inc(meaned.sem, 1)

            def ll_high(b, par, free):
                wait(act, quaded, b, 2)
                if free is not None:
                    wait(act, h_full, free, G)
                nc.scalar.activation(ll_hi[:, :, :], quad[:, par, :, :], ACT.Copy,
                                     scale=-0.25).then_inc(ll_hi_r.sem, 1)

            def hidden(b, g):
                wait(act, h_full, b, g + 1)
                if g >= 2:
                    wait(act, h_lo_r, b, g - 1)
                else:
                    wait(act, h_lo_r, b - 1, G + g - 1)
                nc.scalar.activation(ht[:, g % 2, :], hbank[g % 3][:, :], ACT.Gelu,
                                     bias=fc1b[:, g:g + 1]).then_inc(h_act.sem, 1)
                wait(act, h_act, b, g + 1)
                if g >= 4:
                    wait(act, h_used, b, g - 3)
                else:
                    wait(act, h_used, b - 1, G + g - 3)
                nc.scalar.activation(h_hi[:, g % 4, :], ht[:, g % 2, :], ACT.Copy).then_inc(h_hi_r.sem, 1)

            for h in range(2):
                keep_mean(0, 0, h)
                norm.act_square(act, xb, 0, h)
            for h in range(2):
                norm.act_guess(act, 0, h)
            ll_high(0, 0, None)

            def body(b, par, last, first):
                more = not (last and par)
                for g in range(G):
                    if more and g in MEAN_AT:
                        h = MEAN_AT.index(g)
                        keep_mean(b + 1, 1 - par, h)
                        norm.act_square(act, xb, b + 1, h)
                    if more and g in VAR_AT:
                        norm.act_guess(act, b + 1, VAR_AT.index(g))
                    hidden(b, g)
                if more:
                    ll_high(b + 1, 1 - par, b)

            batches(act, body)

        @block.vector
        def _(dve):
            dve.sem_inc(h_lo_r.sem, G)
            dve.wait_ge(w2_hi_r, 1)
            nc.vector.tensor_tensor(w2_lo[:, :, :], w2_st, w2_hi[:, :, :].bitcast(F32),
                                    ALU.subtract).then_inc(w2_lo_r, 1)
            for i in range(MT * 4):
                m, n = i // 4, i % 4
                dve.wait_ge(w1_hi_r, i + 1)
                nc.vector.tensor_tensor(w1_lo[:, m, n * H:n * H + H], hbank[i % 3][:, :],
                                        w1_hi[:, m, n * H:n * H + H].bitcast(F32),
                                        ALU.subtract).then_inc(w1_lo_r, 1)

            def centre(b, par, h):
                if h == 0:
                    wait(dve, xl, b, 16)
                wait(dve, norm.x_pair, b, h + 1)
                norm.dve_centre(dve, xb, xb, b, h)

            def low_band(b, par, h):
                t = slice(h * H, h * H + H)
                t2 = slice(h * H // 2, h * H // 2 + H // 2)
                norm.dve_newton(dve, b, h)
                wait(dve, norm.inv_dev, b, h + 1)
                wait(dve, paired, b, h + 1)
                nc.vector.tensor_tensor(pairc[:, :, :], pairc[:, :, :],
                                        norm.m2r[:, :].unsqueeze(1).broadcast_to((P, MT, H)),
                                        ALU.mult).then_inc(pair_normed.sem, 1)
                wait(dve, pair_normed, b, h + 1)
                nc.vector.tensor_tensor(quad[:, par, :, t2], pairc[:, :, 0:H:2], pairc[:, :, 1:H:2],
                                        ALU.add).then_inc(quaded.sem, 1)
                nc.vector.tensor_scalar(gain[:, t], norm.m2r[:, :], -0.5, 1.0, ALU.mult,
                                        ALU.add).then_inc(gained.sem, 1)

            def ll_low(b, par):
                wait(dve, ll_hi_r, b, 1)
                wait(dve, quaded, b, 2)
                nc.vector.scalar_tensor_tensor(ll_lo[:, :, :], quad[:, par, :, :], -0.25,
                                               ll_hi[:, :, :].bitcast(F32), ALU.mult,
                                               ALU.subtract).then_inc(ll_lo_r.sem, 1)

            def hidden_low(b, g):
                wait(dve, h_hi_r, b, g + 1)
                nc.vector.tensor_tensor(h_lo[:, g % 4, :], ht[:, g % 2, :], h_hi[:, g % 4, :].bitcast(F32),
                                        ALU.subtract).then_inc(h_lo_r.sem, 1)

            def result_add(b, par):
                wait(dve, h_used, b, G)
                for m in range(MT):
                    nc.vector.scalar_tensor_tensor(change[:, m, :], quad[:, par, m, :], 0.25,
                                                   obank[:, par, m, :], ALU.mult,
                                                   ALU.add).then_inc(changed.sem, 1)
                for m in range(MT):
                    wait(dve, changed, b, m + 1)
                    nc.vector.tensor_scalar(change[:, m, :], change[:, m, :], fc2b[:, m:m + 1], 0.5,
                                            ALU.add, ALU.mult).then_inc(halved.sem, 1)
                wait(dve, meaned, b, 2)
                for m in range(MT):
                    wait(dve, halved, b, m + 1)
                    nc.vector.tensor_tensor(add[:, m, :].rearrange("p (t s) -> p t s", s=2),
                                            change[:, m, :].unsqueeze(2).broadcast_to((P, T2, 2)),
                                            mean[:, par, :].rearrange("p (t s) -> p t s", s=2),
                                            ALU.add).then_inc(added.sem, 1)

            def result(b, par, j):
                wait(dve, added, b, j // 2 + 1)
                wait(dve, scaled, b, j + 1)
                nc.vector.tensor_tensor(zb[:, par, j, :], zb[:, par, j, :], add[:, j // 2, :],
                                        ALU.add).then_inc(z_r.sem, 1)

            for h in range(2):
                centre(0, 0, h)
            for h in range(2):
                low_band(0, 0, h)
            ll_low(0, 0)

            def body(b, par, last, first):
                more = not (last and par)
                for g in range(G):
                    if not first and g == LAG:
                        result_add(b - 1, 1 - par)
                    if not first and g == LAG + 1:
                        for j in range(J):
                            result(b - 1, 1 - par, j)
                    if more and g in MEAN_AT:
                        centre(b + 1, 1 - par, MEAN_AT.index(g))
                    if more and g in VAR_AT:
                        low_band(b + 1, 1 - par, VAR_AT.index(g))
                    hidden_low(b, g)
                if more:
                    ll_low(b + 1, 1 - par)
                else:
                    result_add(b, par)
                    for j in range(J):
                        result(b, par, j)

            batches(dve, body)

        @block.tensor
        def _(pe):
            pe.sem_inc(h_used.sem, G)
            pe.wait_ge(w_in, 80)
            pe.wait_ge(consts, 2)
            for i in range(MT * 4):
                m, n = i // 4, i % 4
                if i >= 3:
                    pe.wait_ge(w1_lo_r, i - 2)
                for c in range(J):
                    last = nc.tensor.matmul(hbank[i % 3][:, :], interp[:, c, m * P:m * P + P],
                                            w1_st[:, c, n * H:n * H + H], start=c == 0, stop=c == J - 1)
                last.then_inc(w1_full, 1)
            pe.wait_ge(w1_lo_r, MT * 4)
            pe.wait_ge(w2_lo_r, 1)
            for h in range(2):
                norm.pe_mean(pe, 0, h, lambda e, b, h: wait(e, meaned, b, h) if h else None)
            wait(pe, meaned, 0, 2)
            for h in range(2):
                norm.pe_var(pe, 0, h)

            def mean_bank_free(e, b, h):
                if h:
                    wait(e, meaned, b, h)
                else:
                    wait(e, norm.guess_err, b - 1, 2)

            def fc1(b, g):
                if g >= 3:
                    wait(pe, h_act, b, g - 2)
                gs = slice(g * P, g * P + P)
                for m in range(MT):
                    last = split3(nc, hbank[g % 3][:, :], w1_hi[:, m, gs], w1_lo[:, m, gs], ll_hi[:, m, :],
                                  ll_lo[:, m, :], m == 0, m == MT - 1)
                last.then_inc(h_full.sem, 1)

            def fc2(b, par, g):
                wait(pe, h_lo_r, b, g + 1)
                for m in range(MT):
                    ms = slice(m * P, m * P + P)
                    last = split3(nc, obank[:, par, m, :], w2_hi[:, g, ms], w2_lo[:, g, ms],
                                  h_hi[:, g % 4, :], h_lo[:, g % 4, :], g == 0, g == G - 1)
                last.then_inc(h_used.sem, 1)

            def body(b, par, last, first):
                more = not (last and par)
                wait(pe, ll_lo_r, b, 1)
                for g in range(G):
                    if more and g in MEAN_PE:
                        norm.pe_mean(pe, b + 1, MEAN_PE.index(g), mean_bank_free)
                    if more and g in VAR_PE:
                        if g == VAR_PE[0]:
                            wait(pe, meaned, b + 1, 2)
                        norm.pe_var(pe, b + 1, VAR_PE.index(g))
                    fc1(b, g)
                    if g >= LAG:
                        fc2(b, par, g - LAG)
                for g in range(G - LAG, G):
                    fc2(b, par, g)

            batches(pe, body)


def program(nc, x, wqkv_t, wproj_t, bproj, fc1_t, fc1_b, interp, fc2_t, fc2_b, scratch, out):
    by_batch = "b (p j) n -> b p j n"
    attention(nc, x.rearrange(by_batch, j=J), wqkv_t, wproj_t, bproj, scratch.rearrange(by_batch, j=J))
    feed_forward(nc, scratch.rearrange(by_batch, j=J), fc1_t, fc1_b, interp, fc2_t, fc2_b,
                 out.rearrange(by_batch, j=J))


def kernel(**inputs):
    import numpy as np
    import concourse.bacc as bacc
    from concourse.bass_utils import run_bass_kernel_spmd

    a = {k: np.ascontiguousarray(v) for k, v in inputs.items()}
    pos = np.arange(C, dtype=np.float32) / np.float32(C - 1) * np.float32(M2 - 1)
    at = np.clip(np.floor(pos).astype(np.int32), 0, M2 - 2)
    frac = (pos - at.astype(np.float32)).astype(np.float32)
    interp = np.zeros((C, M2), np.float32)
    interp[np.arange(C), at] = np.float32(1.0) - frac
    interp[np.arange(C), at + 1] = frac

    def tiles(w):
        return np.ascontiguousarray(w.reshape(-1, P, w.shape[1]).transpose(1, 0, 2))

    def by_tile(w, j):
        return np.ascontiguousarray(w.reshape(w.shape[0], P, j).transpose(0, 2, 1).reshape(w.shape[0], -1))

    arrays = {
        "x": a["x"].reshape(B, C, N),
        "wqkv_t": np.ascontiguousarray(a["L0_conv_w_qkv"].T).reshape(P, J * 3 * C),
        "wproj_t": tiles(by_tile(np.ascontiguousarray(a["L0_conv_w_proj"].T), J)).reshape(P, PAIRS * C),
        "bproj": a["L0_conv_b_proj"].reshape(P, J),
        "fc1_t": tiles(np.ascontiguousarray(a["L0_ffn_fc1_w"].T)),
        "fc1_b": np.ascontiguousarray(a["L0_ffn_fc1_b"].reshape(G, P).T),
        "interp": tiles(by_tile(interp, MT)),
        "fc2_t": tiles(by_tile(np.ascontiguousarray(a["L0_ffn_fc2_w"].T), MT)),
        "fc2_b": a["L0_ffn_fc2_b"].reshape(P, MT),
    }
    nc = bacc.Bacc("TRN2", target_bir_lowering=False, num_devices=1)
    aps = [nc.dram_tensor(f"in_{k}", v.shape, F32, kind="ExternalInput").ap() for k, v in arrays.items()]
    scratch = nc.dram_tensor("x1_scratch", (B, C, N), F32, kind="Internal").ap()
    out = nc.dram_tensor("out_0_dram", (B, C, N), F32, kind="ExternalOutput").ap()
    program(nc, *aps, scratch, out)
    r = run_bass_kernel_spmd(nc, [{f"in_{k}": v for k, v in arrays.items()}], core_ids=[0])
    return r.results[0]["out_0_dram"].reshape(B, C, 32, 32)
```

```python
from contextlib import ExitStack

import concourse.bass as bass
from concourse import mybir

F32 = mybir.dt.float32
F32R = mybir.dt.float32r
F16 = mybir.dt.float16
I32 = mybir.dt.int32
ALU = mybir.AluOpType
ACT = mybir.ActivationFunctionType
AX = mybir.AxisListType
RMAX = bass.bass_isa.ReduceOp.max

P = 128
B = 16
C = 512
J = C // P
N = 1024
H = N // 2
HD = 64
HEADS = C // HD
PAIRS = HEADS // 2
CHUNKS = N // P
HID = 2048
G = HID // P
M2 = C // 2
MT = M2 // P
T2 = N // 2
LN_C_EPS = 1e-6
LN_T_EPS = 1e-5

X_SCALE = 1024.0
E_SCALE = 32768.0
V_SCALE = 2.0 ** -19


MEAN_PE = (6, 7)
VAR_PE = (10, 11)
MEAN_AT = (6, 7)
GUESS_AT = 11
NEWTON_AT = 11
BAND_AT = (12, 13)


class Count:

    def __init__(self, sem, per, primed=False):
        self.sem, self.per, self.primed = sem, per, primed

    def at(self, b, n):
        return (b + (1 if self.primed else 0)) * self.per + n


def wait(eng, count, b, n):
    eng.wait_ge(count.sem, count.at(b, n))


class Norm:

    def __init__(self, nc, ctx, tag, eps, bank, ones):
        def sb(name, shape, dt=F32):
            return ctx.enter_context(nc.sbuf_tensor(f"{name}_{tag}", shape, dt))

        def cnt(name, per):
            return Count(ctx.enter_context(nc.semaphore(f"{name}_{tag}")), per)

        self.nc, self.eps, self.bank, self.ones = nc, eps, bank, ones
        self.banks = bank.shape[1]
        self.units = 2 // self.banks
        self.pair_sum = sb("pair_sum", [P, 2, H])
        self.x_sum = sb("x_sum", [P, 2, H])
        self.sq = sb("sq", [P, J, H])
        self.sq_sum = sb("sq_sum", [P, 2, H])
        self.eps_col = sb("eps_col", [P, 1])
        self.r0 = sb("r0", [P, self.banks * H])
        self.m2r = sb("m2r", [P, self.banks * H])
        self.x_pair = cnt("x_pair", 2)
        self.x_summed = cnt("x_summed", 2)
        self.mean = cnt("mean", 2)
        self.centred = cnt("centred", 2)
        self.squared = cnt("squared", 2)
        self.sq_pair = cnt("sq_pair", 2)
        self.sq_summed = cnt("sq_summed", 2)
        self.var = cnt("var", 2)
        self.logged = cnt("logged", self.units)
        self.guessed = cnt("guessed", self.units)
        self.guess_sq = cnt("guess_sq", self.units)
        self.guess_err = cnt("guess_err", self.units)
        self.inv_dev = cnt("inv_dev", self.units)

    def half_bank(self, h):
        return self.bank[:, h % self.banks, :]

    def unit_bank(self):
        return self.bank[:, :, :].rearrange("p a n -> p (a n)")

    def pool_sum(self, pool, x, b, h):
        t = slice(h * H, h * H + H)
        if h:
            wait(pool, self.x_summed, b, h)
        elif not (isinstance(b, int) and b == 0):
            wait(pool, self.sq_summed, b - 1, 2)
        self.nc.gpsimd.tensor_tensor(self.pair_sum[:, :, :], x[:, 0:2, t], x[:, 2:4, t],
                                     ALU.add).then_inc(self.x_pair.sem, 1)
        wait(pool, self.x_pair, b, h + 1)
        self.nc.gpsimd.tensor_tensor(self.x_sum[:, h, :], self.pair_sum[:, 0, :], self.pair_sum[:, 1, :],
                                     ALU.add).then_inc(self.x_summed.sem, 1)

    def pe_mean(self, pe, b, h):
        wait(pe, self.x_summed, b, h + 1)
        if h and self.banks == 1:
            wait(pe, self.centred, b, h)
        elif not (isinstance(b, int) and b == 0):
            wait(pe, self.guess_err, b - 1, self.units)
        self.nc.tensor.matmul(self.half_bank(h), self.ones[:, :], self.x_sum[:, h, :], start=True,
                              stop=True).then_inc(self.mean.sem, 1)

    def dve_centre(self, dve, x, out, b, h):
        t = slice(h * H, h * H + H)
        wait(dve, self.mean, b, h + 1)
        self.nc.vector.tensor_tensor(out[:, :, t], x[:, :, t],
                                     self.half_bank(h).unsqueeze(1).broadcast_to((P, J, H)),
                                     ALU.subtract).then_inc(self.centred.sem, 1)

    def act_square(self, act, xc, b, h):
        t = slice(h * H, h * H + H)
        wait(act, self.centred, b, h + 1)
        if h:
            wait(act, self.sq_pair, b, h)
        self.nc.scalar.activation(self.sq[:, :, :], xc[:, :, t], ACT.Square).then_inc(self.squared.sem, 1)

    def pool_sq_sum(self, pool, b, h):
        wait(pool, self.squared, b, h + 1)
        if h:
            wait(pool, self.sq_summed, b, h)
        else:
            wait(pool, self.x_summed, b, 2)
        self.nc.gpsimd.tensor_tensor(self.pair_sum[:, :, :], self.sq[:, 0:2, :], self.sq[:, 2:4, :],
                                     ALU.add).then_inc(self.sq_pair.sem, 1)
        wait(pool, self.sq_pair, b, h + 1)
        self.nc.gpsimd.tensor_tensor(self.sq_sum[:, h, :], self.pair_sum[:, 0, :], self.pair_sum[:, 1, :],
                                     ALU.add).then_inc(self.sq_summed.sem, 1)

    def pe_var(self, pe, b, h):
        wait(pe, self.sq_summed, b, h + 1)
        if self.banks == 2:
            wait(pe, self.centred, b, h + 1)
        elif h:
            wait(pe, self.guess_err, b, h)
        else:
            wait(pe, self.centred, b, 2)
        self.nc.tensor.matmul(self.half_bank(h), self.ones[:, :], self.sq_sum[:, h, :], start=True,
                              stop=True).then_inc(self.var.sem, 1)

    def act_guess(self, act, b, u):
        if self.units == 1:
            self.nc.scalar.preload_act_table_set("natural_log_exp_and_others")
        wait(act, self.var, b, 2 if self.units == 1 else u + 1)
        if u:
            wait(act, self.inv_dev, b, u)
        self.nc.scalar.activation(self.r0[:, :], self.unit_bank(), ACT.Ln,
                                  bias=self.eps_col[:, 0:1]).then_inc(self.logged.sem, 1)
        wait(act, self.logged, b, u + 1)
        self.nc.scalar.activation(self.r0[:, :], self.r0[:, :], ACT.Exp,
                                  scale=-0.5).then_inc(self.guessed.sem, 1)

    def dve_newton(self, dve, b, u):
        nc = self.nc
        wait(dve, self.guessed, b, u + 1)
        nc.vector.tensor_tensor(self.m2r[:, :], self.r0[:, :], self.r0[:, :],
                                ALU.mult).then_inc(self.guess_sq.sem, 1)
        wait(dve, self.guess_sq, b, u + 1)
        nc.vector.scalar_tensor_tensor(self.m2r[:, :], self.unit_bank(), self.eps, self.m2r[:, :],
                                       ALU.add, ALU.mult).then_inc(self.guess_err.sem, 1)
        wait(dve, self.guess_err, b, u + 1)
        nc.vector.scalar_tensor_tensor(self.m2r[:, :], self.m2r[:, :], 3.0, self.r0[:, :],
                                       ALU.subtract, ALU.mult).then_inc(self.inv_dev.sem, 1)


def split3(nc, out, a_hi, a_lo, b_hi, b_lo, start, stop, skip=False):
    nc.tensor.matmul(out, a_hi, b_hi, start=start, stop=False, skip_group_check=skip)
    nc.tensor.matmul(out, a_hi, b_lo, start=False, stop=False, skip_group_check=skip)
    return nc.tensor.matmul(out, a_lo, b_hi, start=False, stop=stop, skip_group_check=skip)


def attention(nc, x_dram, wqkv_dram, wproj_dram, bproj_dram, x1_dram):
    ctx = ExitStack()
    with ctx:
        def sb(name, shape, dt=F32):
            return ctx.enter_context(nc.sbuf_tensor(name, shape, dt))

        def sem(name):
            return ctx.enter_context(nc.semaphore(name))

        def cnt(name, per, primed=False):
            return Count(sem(name), per, primed)

        wq_hi = sb("wq_hi", [P, J, 3 * C], F16)
        wq_lo = sb("wq_lo", [P, J, 3 * C], F16)
        wp_hi = sb("wp_hi", [P, PAIRS, C], F32R)
        wp_lo = sb("wp_lo", [P, PAIRS, C], F32R)
        xb = sb("xb", [P, 2, J, N])
        stage = xb[:, :, :, :].rearrange("p a j n -> p (a j n)")
        wq_st = stage[:, 0:J * 3 * C]
        wp_st = stage[:, J * 3 * C:J * 3 * C + PAIRS * C]
        xc = sb("xc", [P, J, N])
        xn_hi = sb("xn_hi", [P, J, N], F16)
        xn_lo = sb("xn_lo", [P, J, N], F16)
        e_tmp = sb("e_tmp", [P, 2, N])
        ek_hi = sb("ek_hi", [P, PAIRS, N], F32R)
        ek_lo = sb("ek_lo", [P, PAIRS, N], F32R)
        eq = sb("eq", [P, 2, C])
        vn = sb("vn", [P, 2, C])
        eq_hi = sb("eq_hi", [P, 2, C], F16)
        eq_lo = sb("eq_lo", [P, 2, C], F16)
        vn_hi = sb("vn_hi", [P, 2, C], F16)
        vn_lo = sb("vn_lo", [P, 2, C], F16)
        qv_hi = sb("qv_hi", [P, PAIRS, P], F32R)
        qv_lo = sb("qv_lo", [P, PAIRS, P], F32R)
        mt_hi = sb("mt_hi", [P, PAIRS, C], F32R)
        mt_lo = sb("mt_lo", [P, PAIRS, C], F32R)
        ones = sb("ones", [P, P])
        bproj = sb("bproj", [P, J])
        small = sb("small", [P, 8])
        row_max, all_max, exp_bits = small[:, 0:1], small[:, 1:2], small[:, 2:3]
        w_scale, un_scale, m_scale = small[:, 3:4], small[:, 4:5], small[:, 5:6]
        k_max = sb("k_max", [P, PAIRS])
        k_bias = sb("k_bias", [P, PAIRS])
        k_sum = sb("k_sum", [P, PAIRS])
        k_inv = sb("k_inv", [P, PAIRS])
        k_gain = sb("k_gain", [P, PAIRS])
        q_max = sb("q_max", [P, 2, HEADS])
        q_sum = sb("q_sum", [P, 2, HEADS])
        q_inv = sb("q_inv", [P, 2, HEADS])

        ring = [ctx.enter_context(nc.psum_tensor(f"ring{i}", [P, 2, H], F32)) for i in range(3)]
        qv_bank = ctx.enter_context(nc.psum_tensor("qv_bank", [P, PAIRS, P], F32))
        nbank = ctx.enter_context(nc.psum_tensor("norm_bank", [P, 1, H], F32))
        norm = Norm(nc, ctx, "a", LN_C_EPS, nbank, ones)

        w_in = sem("w_in")
        prep = sem("prep")
        wq_hi_done = sem("wq_hi_done")
        w_ready = sem("w_ready")
        consts = sem("consts")
        xl = cnt("x_loaded", 16)
        x1_stored = cnt("x1_stored", 32)
        xs = cnt("x_scaled", 2)
        xhi = cnt("xn_hi_ready", 2)
        xlo = cnt("xn_lo_ready", 2)
        k_full = cnt("k_full", PAIRS)
        k_maxed = cnt("k_maxed", PAIRS)
        k_biased = cnt("k_biased", PAIRS)
        k_exp = cnt("k_exp", PAIRS)
        ek_hi_r = cnt("ek_hi_ready", PAIRS)
        ek_lo_r = cnt("ek_lo_ready", PAIRS - 1, True)
        q_full = cnt("q_full", CHUNKS)
        v_full = cnt("v_full", CHUNKS)
        q_maxed = cnt("q_maxed", CHUNKS)
        q_shift = cnt("q_shifted", CHUNKS)
        q_exp = cnt("q_exp", CHUNKS)
        q_summed = cnt("q_summed", CHUNKS)
        q_inved = cnt("q_inverted", CHUNKS)
        v_norm = cnt("v_normed", CHUNKS)
        eq_hi_r = cnt("eq_hi_ready", CHUNKS)
        eq_lo_r = cnt("eq_lo_ready", CHUNKS)
        vn_hi_r = cnt("vn_hi_ready", CHUNKS)
        vn_lo_r = cnt("vn_lo_ready", CHUNKS, True)
        qv_used = cnt("qv_used", CHUNKS, True)
        qv_hi_r = cnt("qv_hi_ready", 2)
        qv_lo_r = cnt("qv_lo_ready", 2, True)
        k_inved = cnt("k_inverted", 2)
        k_gained = cnt("k_gain_ready", 2)
        ek_last = cnt("ek_last_ready", 1, True)
        m_full = cnt("m_full", PAIRS)
        mt_hi_r = cnt("mt_hi_ready", PAIRS)
        mt_lo_r = cnt("mt_lo_ready", PAIRS)
        o_full = cnt("o_full", J, True)
        x1_r = cnt("x1_ready", J, True)

        block = ctx.enter_context(nc.Block())

        def batches(eng, body):
            with eng.Fori(0, B // 2 - 1) as i:
                for par in range(2):
                    body(i * 2 + par, par, False)
            for par in range(2):
                body(B - 2 + par, par, True)

        @block.sync
        def _(sp):
            sp.dma_start(wq_st, wqkv_dram).then_inc(w_in, 16)
            sp.dma_start(wp_st, wproj_dram).then_inc(w_in, 16)
            sp.dma_start(bproj[:, :], bproj_dram).then_inc(w_in, 16)
            sp.wait_ge(w_ready, 4)
            for b in range(2):
                if b:
                    wait(sp, xl, b - 1, 16)
                sp.dma_start(xb[:, b, :, :], x_dram[b]).then_inc(xl.sem, 16)

            def body(b, par, last):
                for half in range(2):
                    j = slice(2 * half, 2 * half + 2)
                    wait(sp, x1_r, b, 2 * half + 2)
                    sp.dma_start(x1_dram[b][:, j, :], xb[:, par, j, :]).then_inc(x1_stored.sem, 16)
                wait(sp, x1_stored, b, 32)
                if not last:
                    sp.dma_start(xb[:, par, :, :], x_dram[b + 2]).then_inc(xl.sem, 16)

            batches(sp, body)

        @block.gpsimd
        def _(pool):
            nc.gpsimd.memset(ones[:, :], 1.0 / C).then_inc(consts, 1)
            nc.gpsimd.memset(norm.eps_col[:, :], LN_C_EPS).then_inc(consts, 1)
            nc.gpsimd.memset(qv_hi[:, :, :].bitcast(F32), 0.0).then_inc(consts, 1)
            nc.gpsimd.memset(qv_lo[:, :, :].bitcast(F32), 0.0).then_inc(consts, 1)
            pool.sem_inc(ek_lo_r.sem, PAIRS - 1)
            pool.sem_inc(vn_lo_r.sem, CHUNKS)
            pool.wait_ge(prep, 1)
            nc.gpsimd.partition_all_reduce(all_max, row_max, P, RMAX).then_inc(prep, 1)

            def norm_sums(b, par):
                wait(pool, xl, b, 16)
                for h in range(2):
                    norm.pool_sum(pool, xb[:, par, :, :], b, h)

            def xn_low(b, h):
                t = slice(h * H, h * H + H)
                wait(pool, xhi, b, h + 1)
                nc.gpsimd.tensor_tensor(xn_lo[:, :, t], xc[:, :, t], xn_hi[:, :, t],
                                        ALU.subtract).then_inc(xlo.sem, 1)

            def k_low(b, j):
                wait(pool, ek_hi_r, b, j + 1)
                nc.gpsimd.tensor_tensor(ek_lo[:, j, :], e_tmp[:, j % 2, :], ek_hi[:, j, :].bitcast(F32),
                                        ALU.subtract).then_inc(ek_lo_r.sem, 1)

            def v_low(b, t):
                wait(pool, vn_hi_r, b, t + 1)
                nc.gpsimd.tensor_tensor(vn_lo[:, t % 2, :], vn[:, t % 2, :], vn_hi[:, t % 2, :],
                                        ALU.subtract).then_inc(vn_lo_r.sem, 1)

            norm_sums(0, 0)
            for h in range(2):
                norm.pool_sq_sum(pool, 0, h)
            for h in range(2):
                xn_low(0, h)

            def body(b, par, last):
                more = not (last and par)
                k_low(b, 0)
                k_low(b, 1)
                if more:
                    norm_sums(b + 1, 1 - par)
                for t in range(1, CHUNKS):
                    v_low(b, t - 1)
                    if more and t in (4, 5):
                        norm.pool_sq_sum(pool, b + 1, t - 4)
                v_low(b, CHUNKS - 1)
                k_low(b, 2)
                if more:
                    for h in range(2):
                        xn_low(b + 1, h)

            batches(pool, body)

        @block.scalar
        def _(act):
            nc.scalar.preload_act_table_set("natural_log_exp_and_others")
            act.wait_ge(consts, 4)
            act.wait_ge(prep, 5)
            nc.scalar.activation(wq_hi[:, :, :], wq_st.rearrange("p (j n) -> p j n", j=J), ACT.Copy,
                                 scale=w_scale).then_inc(wq_hi_done, 1)
            nc.scalar.activation(wp_hi[:, :, :], wp_st.rearrange("p (j n) -> p j n", j=PAIRS),
                                 ACT.Copy).then_inc(wq_hi_done, 1)

            def xn_high(b, h, free):
                t = slice(h * H, h * H + H)
                wait(act, xs, b, h + 1)
                if free is not None:
                    wait(act, k_full, free, PAIRS)
                nc.scalar.activation(xn_hi[:, :, t], xc[:, :, t], ACT.Copy).then_inc(xhi.sem, 1)

            def k_tile(b, j, s):
                wait(act, k_biased, b, j + 1)
                if j == 0:
                    wait(act, ek_lo_r, b - 1, 3)
                elif j == 1:
                    wait(act, ek_last, b - 1, 1)
                else:
                    wait(act, ek_lo_r, b, j - 1)
                nc.scalar.activation(e_tmp[:, j % 2, :], ring[s % 3][:, :, :].rearrange("p a n -> p (a n)"),
                                     ACT.Exp, bias=k_bias[:, j:j + 1], scale=un_scale,
                                     accum_out=k_sum[:, j:j + 1]).then_inc(k_exp.sem, 1)

            def k_high(b, j):
                wait(act, k_exp, b, j + 1)
                wait(act, o_full, b - 1, J)
                nc.scalar.activation(ek_hi[:, j, :], e_tmp[:, j % 2, :], ACT.Copy).then_inc(ek_hi_r.sem, 1)

            def q_high(b, t):
                wait(act, q_shift, b, t + 1)
                nc.scalar.activation(eq[:, t % 2, :], eq[:, t % 2, :], ACT.Exp,
                                     scale=un_scale).then_inc(q_exp.sem, 1)
                wait(act, q_exp, b, t + 1)
                if t < 2:
                    wait(act, qv_used, b - 1, t + 7)
                else:
                    wait(act, qv_used, b, t - 1)
                nc.scalar.activation(eq_hi[:, t % 2, :], eq[:, t % 2, :], ACT.Copy,
                                     scale=E_SCALE).then_inc(eq_hi_r.sem, 1)

            def v_high(b, t):
                wait(act, v_norm, b, t + 1)
                nc.scalar.activation(vn_hi[:, t % 2, :], vn[:, t % 2, :], ACT.Copy).then_inc(vn_hi_r.sem, 1)

            for h in range(2):
                norm.act_square(act, xc, 0, h)
            for h in range(2):
                norm.act_guess(act, 0, h)
            for h in range(2):
                xn_high(0, h, None)

            def body(b, par, last):
                more = not (last and par)
                for j in range(2):
                    k_tile(b, j, j)
                    k_high(b, j)
                for t in range(CHUNKS):
                    if more and t in (6, 7):
                        norm.act_guess(act, b + 1, t - 6)
                    q_high(b, t)
                    if t:
                        v_high(b, t - 1)
                    if more and t in (3, 4):
                        norm.act_square(act, xc, b + 1, t - 3)
                v_high(b, CHUNKS - 1)
                k_tile(b, 2, 10)
                k_high(b, 2)
                wait(act, qv_used, b, CHUNKS)
                for d in range(2):
                    s = slice(d * HD, d * HD + HD)
                    nc.scalar.activation(qv_hi[s, :, s], qv_bank[s, :, s], ACT.Copy).then_inc(qv_hi_r.sem, 1)
                for p in range(PAIRS):
                    if p == 2:
                        k_tile(b, 3, 11)
                    if p == 3:
                        k_high(b, 3)
                    wait(act, m_full, b, p + 1)
                    if p in (0, 3):
                        wait(act, k_gained, b, 1 + p // 3)
                    nc.scalar.activation(mt_hi[:, p, :], ring[(12 + p // 2) % 3][:, p % 2, :], ACT.Copy,
                                         scale=k_gain[:, p:p + 1]).then_inc(mt_hi_r.sem, 1)
                if more:
                    for h in range(2):
                        xn_high(b + 1, h, b)

            batches(act, body)

        @block.vector
        def _(dve):
            dve.wait_ge(w_in, 48)
            nc.vector.tensor_reduce(row_max, wq_st, AX.X, ALU.max, apply_absolute_value=True).then_inc(prep, 1)
            dve.wait_ge(prep, 2)
            nc.vector.tensor_scalar_max(exp_bits, all_max, 1e-30).then_inc(prep, 1)
            dve.wait_ge(prep, 3)
            nc.vector.tensor_scalar(exp_bits.bitcast(I32), exp_bits.bitcast(I32), 0x7F800000, None,
                                    ALU.bitwise_and).then_inc(prep, 1)
            dve.wait_ge(prep, 4)
            nc.vector.tensor_scalar(un_scale.bitcast(I32), exp_bits.bitcast(I32), 1.0, float(-24 * 2 ** 23),
                                    ALU.mult, ALU.add)
            nc.vector.tensor_scalar(m_scale.bitcast(I32), exp_bits.bitcast(I32), 1.0, float(-20 * 2 ** 23),
                                    ALU.mult, ALU.add)
            nc.vector.tensor_scalar(w_scale.bitcast(I32), exp_bits.bitcast(I32), -1.0, float(268 * 2 ** 23),
                                    ALU.mult, ALU.add).then_inc(prep, 1)
            dve.wait_ge(prep, 5)
            dve.sem_inc(x1_r.sem, J)
            dve.sem_inc(ek_last.sem, 1)
            dve.sem_inc(qv_lo_r.sem, 2)
            dve.wait_ge(wq_hi_done, 1)
            nc.vector.scalar_tensor_tensor(wq_lo[:, :, :].rearrange("p j n -> p (j n)"), wq_st, w_scale,
                                           wq_hi[:, :, :].rearrange("p j n -> p (j n)"), ALU.mult,
                                           ALU.subtract).then_inc(w_ready, 2)
            dve.wait_ge(wq_hi_done, 2)
            nc.vector.tensor_tensor(wp_lo[:, :, :].rearrange("p j n -> p (j n)"), wp_st,
                                    wp_hi[:, :, :].rearrange("p j n -> p (j n)").bitcast(F32),
                                    ALU.subtract).then_inc(w_ready, 2)

            def newton(b, h):
                if h:
                    wait(dve, xs, b, h)
                elif not (isinstance(b, int) and b == 0):
                    wait(dve, xs, b - 1, 2)
                norm.dve_newton(dve, b, h)

            def x_scale(b, h):
                t = slice(h * H, h * H + H)
                wait(dve, norm.inv_dev, b, h + 1)
                wait(dve, norm.squared, b, h + 1)
                nc.vector.scalar_tensor_tensor(
                    xc[:, :, t], xc[:, :, t], -0.5 * X_SCALE,
                    norm.m2r[:, :].unsqueeze(1).broadcast_to((P, J, H)), ALU.mult, ALU.mult).then_inc(xs.sem, 1)

            def centre(b, par, h):
                if h == 0:
                    wait(dve, xl, b, 16)
                dve_free = b
                norm.dve_centre(dve, xb[:, par, :, :], xc, dve_free, h)

            def k_tile(b, j, s):
                wait(dve, k_full, b, j + 1)
                nc.vector.reduce_max(k_max[:, j:j + 1], ring[s % 3][:, :, :].rearrange("p a n -> p (a n)"),
                                     AX.X).then_inc(k_maxed.sem, 1)
                wait(dve, k_maxed, b, j + 1)
                nc.vector.tensor_scalar(k_bias[:, j:j + 1], k_max[:, j:j + 1], un_scale, -1.0, ALU.mult,
                                        ALU.mult).then_inc(k_biased.sem, 1)

            def heads(ap):
                return ap.rearrange("p (h d) -> p h d", h=HEADS)

            def spread(ap):
                return ap.unsqueeze(2).broadcast_to((P, HEADS, HD))

            def q_shift_chunk(b, t):
                bank = ring[(t + 2) % 3][:, 0, :]
                wait(dve, q_full, b, t + 1)
                nc.vector.reduce_max(q_max[:, t % 2, :], heads(bank), AX.X).then_inc(q_maxed.sem, 1)
                wait(dve, q_maxed, b, t + 1)
                if t >= 2:
                    wait(dve, eq_hi_r, b, t - 1)
                nc.vector.tensor_tensor(heads(eq[:, t % 2, :]), heads(bank), spread(q_max[:, t % 2, :]),
                                        ALU.subtract).then_inc(q_shift.sem, 1)

            def v_chunk(b, t):
                bank = ring[(t + 2) % 3][:, 1, :]
                wait(dve, q_exp, b, t + 1)
                nc.vector.reduce_sum(q_sum[:, t % 2, :], heads(eq[:, t % 2, :]), AX.X).then_inc(q_summed.sem, 1)
                wait(dve, q_summed, b, t + 1)
                nc.vector.reciprocal(q_inv[:, t % 2, :], q_sum[:, t % 2, :]).then_inc(q_inved.sem, 1)
                wait(dve, q_inved, b, t + 1)
                wait(dve, v_full, b, t + 1)
                if t >= 2:
                    wait(dve, vn_lo_r, b, t - 1)
                else:
                    wait(dve, vn_lo_r, b - 1, t + 7)
                nc.vector.scalar_tensor_tensor(heads(vn[:, t % 2, :]), heads(bank), V_SCALE,
                                               spread(q_inv[:, t % 2, :]), ALU.mult,
                                               ALU.mult).then_inc(v_norm.sem, 1)

            def q_low(b, t):
                wait(dve, eq_hi_r, b, t + 1)
                nc.vector.scalar_tensor_tensor(eq_lo[:, t % 2, :], eq[:, t % 2, :], E_SCALE,
                                               eq_hi[:, t % 2, :], ALU.mult,
                                               ALU.subtract).then_inc(eq_lo_r.sem, 1)

            for h in range(2):
                centre(0, 0, h)
            for h in range(2):
                newton(0, h)
                x_scale(0, h)

            def body(b, par, last):
                more = not (last and par)
                k_tile(b, 0, 0)
                k_tile(b, 1, 1)
                for t in range(CHUNKS):
                    if more and t in (3, 4):
                        if t == 3:
                            wait(dve, xlo, b, 2)
                        centre(b + 1, 1 - par, t - 3)
                    q_shift_chunk(b, t)
                    if more and t in (6, 7):
                        newton(b + 1, t - 6)
                    if t:
                        v_chunk(b, t - 1)
                        q_low(b, t - 1)
                    if more and t in (6, 7):
                        x_scale(b + 1, t - 6)
                v_chunk(b, CHUNKS - 1)
                q_low(b, CHUNKS - 1)
                k_tile(b, 2, 10)
                for d in range(2):
                    s = slice(d * HD, d * HD + HD)
                    wait(dve, qv_hi_r, b, 2)
                    nc.vector.tensor_tensor(qv_lo[s, :, s], qv_bank[s, :, s], qv_hi[s, :, s].bitcast(F32),
                                            ALU.subtract).then_inc(qv_lo_r.sem, 1)

                def k_gains(n, js):
                    wait(dve, k_exp, b, js.stop)
                    nc.vector.reciprocal(k_inv[:, js], k_sum[:, js]).then_inc(k_inved.sem, 1)
                    wait(dve, k_inved, b, n)
                    nc.vector.tensor_scalar(k_gain[:, js], k_inv[:, js], m_scale, None,
                                            ALU.mult).then_inc(k_gained.sem, 1)

                k_gains(1, slice(0, 3))
                k_tile(b, 3, 11)
                for p in range(PAIRS):
                    if p == 3:
                        k_gains(2, slice(3, 4))
                        wait(dve, ek_hi_r, b, PAIRS)
                        nc.vector.tensor_tensor(ek_lo[:, 3, :], e_tmp[:, 1, :], ek_hi[:, 3, :].bitcast(F32),
                                                ALU.subtract).then_inc(ek_last.sem, 1)
                    if p in (0, 3):
                        wait(dve, k_gained, b, 1 + p // 3)
                    wait(dve, mt_hi_r, b, p + 1)
                    nc.vector.scalar_tensor_tensor(mt_lo[:, p, :], ring[(12 + p // 2) % 3][:, p % 2, :],
                                                   k_gain[:, p:p + 1], mt_hi[:, p, :].bitcast(F32),
                                                   ALU.mult, ALU.subtract).then_inc(mt_lo_r.sem, 1)
                for j in range(J):
                    wait(dve, o_full, b, j + 1)
                    nc.vector.scalar_tensor_tensor(
                        xb[:, par, j, :], ring[(14 + j) % 3][:, :, :].rearrange("p a n -> p (a n)"),
                        bproj[:, j:j + 1], xb[:, par, j, :], ALU.add, ALU.add).then_inc(x1_r.sem, 1)

            batches(dve, body)

        @block.tensor
        def _(pe):
            pe.sem_inc(o_full.sem, J)
            pe.sem_inc(qv_used.sem, CHUNKS)
            pe.wait_ge(consts, 4)
            pe.wait_ge(w_ready, 4)

            def k_half(b, j, s, h):
                t = slice(h * H, h * H + H)
                w = slice(C + j * P, C + j * P + P)
                for c in range(J):
                    last = split3(nc, ring[s % 3][:, h, :], wq_hi[:, c, w], wq_lo[:, c, w], xn_hi[:, c, t],
                                  xn_lo[:, c, t], c == 0, c == J - 1)
                return last

            def chunk(b, t):
                ts = slice(t * P, t * P + P)
                for part, count in ((0, q_full), (1, v_full)):
                    w = slice(part * 2 * C, part * 2 * C + C)
                    for c in range(J):
                        last = split3(nc, ring[(t + 2) % 3][:, part, :], xn_hi[:, c, ts], xn_lo[:, c, ts],
                                      wq_hi[:, c, w], wq_lo[:, c, w], c == 0, c == J - 1)
                    last.then_inc(count.sem, 1)

            def qv_chunk(b, t):
                wait(pe, eq_lo_r, b, t + 1)
                wait(pe, vn_lo_r, b, t + 1)
                if t == 0:
                    wait(pe, qv_lo_r, b - 1, 2)
                i = t % 2
                for p in range(PAIRS):
                    s = slice(p * P, p * P + P)
                    last = split3(nc, qv_bank[:, p, :], eq_hi[:, i, s], eq_lo[:, i, s], vn_hi[:, i, s],
                                  vn_lo[:, i, s], t == 0 and p == 0, t == CHUNKS - 1, True)
                last.then_inc(qv_used.sem, 1)

            for h in range(2):
                norm.pe_mean(pe, 0, h)
            for h in range(2):
                norm.pe_var(pe, 0, h)

            def body(b, par, last):
                more = not (last and par)
                wait(pe, xlo, b, 2)
                wait(pe, x1_r, b - 1, 2)
                for h in range(2):
                    k = k_half(b, 0, 0, h)
                k.then_inc(k_full.sem, 1)
                wait(pe, x1_r, b - 1, 3)
                for h in range(2):
                    k = k_half(b, 1, 1, h)
                k.then_inc(k_full.sem, 1)
                for t in range(CHUNKS):
                    if t == 0:
                        wait(pe, x1_r, b - 1, 4)
                    elif t < 3:
                        wait(pe, k_exp, b, t)
                    else:
                        wait(pe, v_norm, b, t - 2)
                    chunk(b, t)
                    if t >= 2:
                        qv_chunk(b, t - 2)
                    if more and t in (2, 3):
                        norm.pe_mean(pe, b + 1, t - 2)
                    if more and t in (5, 6):
                        norm.pe_var(pe, b + 1, t - 5)
                wait(pe, v_norm, b, 6)
                for h in range(2):
                    k = k_half(b, 2, 10, h)
                k.then_inc(k_full.sem, 1)
                qv_chunk(b, 6)
                wait(pe, v_norm, b, 7)
                k_half(b, 3, 11, 0)
                qv_chunk(b, 7)
                k_half(b, 3, 11, 1).then_inc(k_full.sem, 1)
                wait(pe, qv_lo_r, b, 2)
                for p in range(PAIRS):
                    if p == 0:
                        wait(pe, v_norm, b, 8)
                    if p == 2:
                        wait(pe, k_exp, b, 3)
                    split3(nc, ring[(12 + p // 2) % 3][:, p % 2, :], qv_hi[:, p, :], qv_lo[:, p, :],
                           wp_hi[:, p, :], wp_lo[:, p, :], True, True).then_inc(m_full.sem, 1)
                for j in range(J):
                    if j == 0:
                        wait(pe, k_exp, b, 4)
                    elif j == 3:
                        wait(pe, x1_r, b, 1)
                    js = slice(j * P, j * P + P)
                    for p in range(PAIRS):
                        if j == 0:
                            wait(pe, mt_lo_r, b, p + 1)
                            if p < 3:
                                wait(pe, ek_lo_r, b, p + 1)
                            else:
                                wait(pe, ek_last, b, 1)
                        for h in range(2):
                            t = slice(h * H, h * H + H)
                            last = split3(nc, ring[(14 + j) % 3][:, h, :], mt_hi[:, p, js], mt_lo[:, p, js],
                                          ek_hi[:, p, t], ek_lo[:, p, t], p == 0, p == PAIRS - 1)
                    last.then_inc(o_full.sem, 1)

            batches(pe, body)


def feed_forward(nc, x1_dram, fc1t_dram, fc1b_dram, interp_dram, fc2t_dram, fc2b_dram, out_dram):
    ctx = ExitStack()
    with ctx:
        def sb(name, shape, dt=F32):
            return ctx.enter_context(nc.sbuf_tensor(name, shape, dt))

        def sem(name):
            return ctx.enter_context(nc.semaphore(name))

        def cnt(name, per, primed=False):
            return Count(sem(name), per, primed)

        LAG = 3
        HB = 4
        w1_hi = sb("w1_hi", [P, MT, HID], F32R)
        w1_lo = sb("w1_lo", [P, MT, HID], F32R)
        w2_hi = sb("w2_hi", [P, G, M2], F32R)
        w2_lo = sb("w2_lo", [P, G, M2], F32R)
        xb = sb("fx", [P, J, N])
        zb = sb("zb", [P, 2, J, N])
        w1_st = zb[:, :, :, :].rearrange("p a j n -> p (a j n)").rearrange("p (j n) -> p j n", j=J)
        w2_st = xb[:, :, :].rearrange("p j n -> p (j n)").rearrange("p (g m) -> p g m", g=G)
        ones = sb("f_ones", [P, P])
        fc1b = sb("fc1b", [P, G])
        fc2b = sb("fc2b", [P, MT])
        mean = sb("mean_row", [P, 2, N])
        gain = sb("gain", [P, N])
        pairc = sb("pairc", [P, MT, H])
        quad = sb("quad", [P, 2, MT, T2])
        ll_hi = sb("ll_hi", [P, MT, T2], F32R)
        ll_lo = sb("ll_lo", [P, MT, T2], F32R)
        ht = sb("ht", [P, 2, T2])
        h_hi = sb("h_hi", [P, 4, T2], F32R)
        h_lo = sb("h_lo", [P, 4, T2], F32R)
        change = sb("change", [P, MT, T2])
        add = sb("add", [P, MT, N])
        interp = add[:, 0, :].rearrange("p (j m) -> p j m", j=J)

        hbank = [ctx.enter_context(nc.psum_tensor(f"hbank{i}", [P, T2], F32)) for i in range(HB)]
        obank = ctx.enter_context(nc.psum_tensor("obank", [P, MT, T2], F32))
        nbank = ctx.enter_context(nc.psum_tensor("f_norm_bank", [P, 2, H], F32))
        norm = Norm(nc, ctx, "b", LN_T_EPS, nbank, ones)

        w_in = sem("f_w_in")
        consts = sem("f_consts")
        w1_full = sem("w1_full")
        w1_hi_r = sem("w1_hi_ready")
        w1_lo_r = sem("w1_lo_ready")
        w2_hi_r = sem("w2_hi_ready")
        w2_lo_r = sem("w2_lo_ready")
        xl = cnt("f_x_loaded", 16)
        meaned = cnt("mean_kept", 2)
        paired = cnt("channel_pairs", 2)
        pair_normed = cnt("pairs_normed", 2)
        quaded = cnt("quads", 2)
        ll_hi_r = cnt("ll_hi_ready", 1)
        ll_lo_r = cnt("ll_lo_ready", 1)
        gained = cnt("gain_ready", 1)
        scaled = cnt("x_gained", 4)
        h_full = cnt("h_full", G)
        h_act = cnt("h_gelu", G)
        h_hi_r = cnt("h_hi_ready", G)
        h_lo_r = cnt("h_lo_ready", G, True)
        h_used = cnt("h_used", G, True)
        changed = cnt("change_raw", MT)
        halved = cnt("change_ready", MT)
        added = cnt("add_ready", MT)
        z_r = cnt("z_ready", J)
        z_stored = [cnt(f"z_stored{par}", 16) for par in range(2)]

        block = ctx.enter_context(nc.Block())

        def batches(eng, body):
            for par in range(2):
                body(par, par, False, par == 0)
            with eng.Fori(1, B // 2 - 1) as i:
                for par in range(2):
                    body(i * 2 + par, par, False, False)
            for par in range(2):
                body(B - 2 + par, par, True, False)

        @block.sync
        def _(sp):
            sp.dma_start(w1_st, fc1t_dram).then_inc(w_in, 16)
            sp.dma_start(interp[:, :, :], interp_dram).then_inc(w_in, 16)
            sp.dma_start(w2_st, fc2t_dram).then_inc(w_in, 16)
            sp.dma_start(fc1b[:, :], fc1b_dram).then_inc(w_in, 16)
            sp.dma_start(fc2b[:, :], fc2b_dram).then_inc(w_in, 16)
            sp.wait_ge(w2_lo_r, 1)
            sp.dma_start(xb[:, :, :], x1_dram[0]).then_inc(xl.sem, 16)

            def store(b, par):
                for half in range(2):
                    j = slice(2 * half, 2 * half + 2)
                    wait(sp, z_r, b, 2 * half + 2)
                    sp.dma_start(out_dram[b][:, j, :], zb[:, par, j, :]).then_inc(z_stored[par].sem, 16)

            def body(b, par, last, first):
                if not (last and par):
                    wait(sp, scaled, b, J)
                    sp.dma_start(xb[:, :, :], x1_dram[b + 1]).then_inc(xl.sem, 16)
                if not first:
                    store(b - 1, 1 - par)
                if last and par:
                    store(b, par)
                    for k in range(2):
                        wait(sp, z_stored[k], b - par, 32)

            batches(sp, body)

        @block.gpsimd
        def _(pool):
            nc.gpsimd.memset(ones[:, :], 1.0 / C).then_inc(consts, 1)
            nc.gpsimd.memset(norm.eps_col[:, :], LN_T_EPS).then_inc(consts, 1)

            def sums(b, par):
                wait(pool, xl, b, 16)
                for h in range(2):
                    norm.pool_sum(pool, xb, b, h)

            def pair(b, par, h):
                t = slice(h * H, h * H + H)
                wait(pool, norm.centred, b, h + 1)
                if h:
                    wait(pool, quaded, b, h)
                nc.gpsimd.tensor_tensor(pairc[:, :, :], xb[:, 0:4:2, t], xb[:, 1:4:2, t],
                                        ALU.add).then_inc(paired.sem, 1)

            def gains(b, par, j):
                wait(pool, gained, b, 1)
                if not (isinstance(b, int) and b < 2):
                    wait(pool, z_stored[par], b - par - 2, 32)
                nc.gpsimd.tensor_tensor(zb[:, par, j, :], xb[:, j, :], gain[:, :],
                                        ALU.mult).then_inc(scaled.sem, 1)

            def pre(b, par):
                sums(b, par)
                for h in range(2):
                    norm.pool_sq_sum(pool, b, h)
                    pair(b, par, h)
                for j in range(J):
                    gains(b, par, j)

            pool.wait_ge(w1_full, MT * 4)
            pre(0, 0)

            def body(b, par, last, first):
                if not (last and par):
                    pre(b + 1, 1 - par)

            batches(pool, body)

        @block.scalar
        def _(act):
            act.wait_ge(consts, 2)
            act.wait_ge(w_in, 80)
            nc.scalar.activation(w2_hi[:, :, :], w2_st, ACT.Copy).then_inc(w2_hi_r, 1)
            for i in range(MT * 4):
                m, n = i // 4, i % 4
                act.wait_ge(w1_full, i + 1)
                nc.scalar.activation(w1_hi[:, m, n * H:n * H + H], hbank[i % HB][:, :],
                                     ACT.Copy).then_inc(w1_hi_r, 1)

            def keep_mean(b, par, h):
                wait(act, norm.centred, b, h + 1)
                nc.scalar.activation(mean[:, par, h * H:h * H + H], nbank[:, h, :], ACT.Copy).then_inc(meaned.sem, 1)

            def ll_high(b, par, free):
                wait(act, quaded, b, 2)
                if free is not None:
                    wait(act, h_full, free, G)
                nc.scalar.activation(ll_hi[:, :, :], quad[:, par, :, :], ACT.Copy,
                                     scale=-0.25).then_inc(ll_hi_r.sem, 1)

            def hidden(b, g):
                wait(act, h_full, b, g + 1)
                if g >= 2:
                    wait(act, h_lo_r, b, g - 1)
                else:
                    wait(act, h_lo_r, b - 1, G + g - 1)
                nc.scalar.activation(ht[:, g % 2, :], hbank[g % HB][:, :], ACT.Gelu,
                                     bias=fc1b[:, g:g + 1]).then_inc(h_act.sem, 1)
                wait(act, h_act, b, g + 1)
                if g >= 4:
                    wait(act, h_used, b, g - 3)
                else:
                    wait(act, h_used, b - 1, G + g - 3)
                nc.scalar.activation(h_hi[:, g % 4, :], ht[:, g % 2, :], ACT.Copy).then_inc(h_hi_r.sem, 1)

            for h in range(2):
                keep_mean(0, 0, h)
                norm.act_square(act, xb, 0, h)
            norm.act_guess(act, 0, 0)
            ll_high(0, 0, None)

            def body(b, par, last, first):
                more = not (last and par)
                for g in range(G):
                    if more and g in MEAN_AT:
                        h = MEAN_AT.index(g)
                        keep_mean(b + 1, 1 - par, h)
                        norm.act_square(act, xb, b + 1, h)
                    if more and g == GUESS_AT:
                        norm.act_guess(act, b + 1, 0)
                    hidden(b, g)
                if more:
                    ll_high(b + 1, 1 - par, b)

            batches(act, body)

        @block.vector
        def _(dve):
            dve.sem_inc(h_lo_r.sem, G)
            dve.wait_ge(w2_hi_r, 1)
            nc.vector.tensor_tensor(w2_lo[:, :, :], w2_st, w2_hi[:, :, :].bitcast(F32),
                                    ALU.subtract).then_inc(w2_lo_r, 1)
            for i in range(MT * 4):
                m, n = i // 4, i % 4
                dve.wait_ge(w1_hi_r, i + 1)
                nc.vector.tensor_tensor(w1_lo[:, m, n * H:n * H + H], hbank[i % HB][:, :],
                                        w1_hi[:, m, n * H:n * H + H].bitcast(F32),
                                        ALU.subtract).then_inc(w1_lo_r, 1)

            def centre(b, par, h):
                if h == 0:
                    wait(dve, xl, b, 16)
                wait(dve, norm.x_pair, b, h + 1)
                norm.dve_centre(dve, xb, xb, b, h)

            def gain_row(b):
                nc.vector.tensor_scalar(gain[:, :], norm.m2r[:, :], -0.5, 1.0, ALU.mult,
                                        ALU.add).then_inc(gained.sem, 1)

            def low_band(b, par, h):
                t = slice(h * H, h * H + H)
                t2 = slice(h * H // 2, h * H // 2 + H // 2)
                wait(dve, norm.inv_dev, b, 1)
                wait(dve, paired, b, h + 1)
                nc.vector.tensor_tensor(pairc[:, :, :], pairc[:, :, :],
                                        norm.m2r[:, t].unsqueeze(1).broadcast_to((P, MT, H)),
                                        ALU.mult).then_inc(pair_normed.sem, 1)
                if h == 0:
                    gain_row(b)
                wait(dve, pair_normed, b, h + 1)
                nc.vector.tensor_tensor(quad[:, par, :, t2], pairc[:, :, 0:H:2], pairc[:, :, 1:H:2],
                                        ALU.add).then_inc(quaded.sem, 1)

            def ll_low(b, par):
                wait(dve, ll_hi_r, b, 1)
                wait(dve, quaded, b, 2)
                nc.vector.scalar_tensor_tensor(ll_lo[:, :, :], quad[:, par, :, :], -0.25,
                                               ll_hi[:, :, :].bitcast(F32), ALU.mult,
                                               ALU.subtract).then_inc(ll_lo_r.sem, 1)

            def hidden_low(b, g):
                wait(dve, h_hi_r, b, g + 1)
                nc.vector.tensor_tensor(h_lo[:, g % 4, :], ht[:, g % 2, :], h_hi[:, g % 4, :].bitcast(F32),
                                        ALU.subtract).then_inc(h_lo_r.sem, 1)

            def result_change(b, par):
                wait(dve, h_used, b, G)
                for m in range(MT):
                    nc.vector.scalar_tensor_tensor(change[:, m, :], quad[:, par, m, :], 0.25,
                                                   obank[:, m, :], ALU.mult,
                                                   ALU.add).then_inc(changed.sem, 1)
                for m in range(MT):
                    wait(dve, changed, b, m + 1)
                    nc.vector.tensor_scalar(change[:, m, :], change[:, m, :], fc2b[:, m:m + 1], 0.5,
                                            ALU.add, ALU.mult).then_inc(halved.sem, 1)

            def result_add(b, par):
                wait(dve, meaned, b, 2)
                for m in range(MT):
                    wait(dve, halved, b, m + 1)
                    nc.vector.tensor_tensor(add[:, m, :].rearrange("p (t s) -> p t s", s=2),
                                            change[:, m, :].unsqueeze(2).broadcast_to((P, T2, 2)),
                                            mean[:, par, :].rearrange("p (t s) -> p t s", s=2),
                                            ALU.add).then_inc(added.sem, 1)

            def result(b, par, j):
                wait(dve, added, b, j // 2 + 1)
                wait(dve, scaled, b, j + 1)
                nc.vector.tensor_tensor(zb[:, par, j, :], zb[:, par, j, :], add[:, j // 2, :],
                                        ALU.add).then_inc(z_r.sem, 1)

            for h in range(2):
                centre(0, 0, h)
            norm.dve_newton(dve, 0, 0)
            for h in range(2):
                low_band(0, 0, h)
            ll_low(0, 0)

            def body(b, par, last, first):
                more = not (last and par)
                for g in range(G):
                    if not first and g == 0:
                        result_change(b - 1, 1 - par)
                    if not first and g == 1:
                        result_add(b - 1, 1 - par)
                    if not first and g in (2, 3):
                        for j in range(2 * g - 4, 2 * g - 2):
                            result(b - 1, 1 - par, j)
                    if more and g in MEAN_AT:
                        centre(b + 1, 1 - par, MEAN_AT.index(g))
                    if more and g == NEWTON_AT:
                        norm.dve_newton(dve, b + 1, 0)
                    if more and g in BAND_AT:
                        low_band(b + 1, 1 - par, BAND_AT.index(g))
                    hidden_low(b, g)
                if more:
                    ll_low(b + 1, 1 - par)
                else:
                    result_change(b, par)
                    result_add(b, par)
                    for j in range(J):
                        result(b, par, j)

            batches(dve, body)

        @block.tensor
        def _(pe):
            pe.sem_inc(h_used.sem, G)
            pe.wait_ge(w_in, 80)
            pe.wait_ge(consts, 2)
            for i in range(MT * 4):
                m, n = i // 4, i % 4
                if i >= HB:
                    pe.wait_ge(w1_lo_r, i - HB + 1)
                for c in range(J):
                    last = nc.tensor.matmul(hbank[i % HB][:, :], interp[:, c, m * P:m * P + P],
                                            w1_st[:, c, n * H:n * H + H], start=c == 0, stop=c == J - 1)
                last.then_inc(w1_full, 1)
            pe.wait_ge(w1_lo_r, MT * 4)
            pe.wait_ge(w2_lo_r, 1)
            for h in range(2):
                norm.pe_mean(pe, 0, h)
            wait(pe, meaned, 0, 2)
            for h in range(2):
                norm.pe_var(pe, 0, h)

            def fc1(b, g):
                if g >= HB:
                    wait(pe, h_act, b, g - HB + 1)
                gs = slice(g * P, g * P + P)
                for m in range(MT):
                    last = split3(nc, hbank[g % HB][:, :], w1_hi[:, m, gs], w1_lo[:, m, gs], ll_hi[:, m, :],
                                  ll_lo[:, m, :], m == 0, m == MT - 1)
                last.then_inc(h_full.sem, 1)

            def fc2(b, g, first):
                wait(pe, h_lo_r, b, g + 1)
                if g == 0 and not first:
                    wait(pe, changed, b - 1, MT)
                for m in range(MT):
                    ms = slice(m * P, m * P + P)
                    last = split3(nc, obank[:, m, :], w2_hi[:, g, ms], w2_lo[:, g, ms],
                                  h_hi[:, g % 4, :], h_lo[:, g % 4, :], g == 0, g == G - 1)
                last.then_inc(h_used.sem, 1)

            def body(b, par, last, first):
                more = not (last and par)
                wait(pe, ll_lo_r, b, 1)
                for g in range(G):
                    if more and g in MEAN_PE:
                        norm.pe_mean(pe, b + 1, MEAN_PE.index(g))
                    if more and g in VAR_PE:
                        if g == VAR_PE[0]:
                            wait(pe, meaned, b + 1, 2)
                        norm.pe_var(pe, b + 1, VAR_PE.index(g))
                    fc1(b, g)
                    if g >= LAG:
                        fc2(b, g - LAG, first)
                for g in range(G - LAG, G):
                    fc2(b, g, first)

            batches(pe, body)


def program(nc, x, wqkv_t, wproj_t, bproj, fc1_t, fc1_b, interp, fc2_t, fc2_b, scratch, out):
    by_batch = "b (p j) n -> b p j n"
    attention(nc, x.rearrange(by_batch, j=J), wqkv_t, wproj_t, bproj, scratch.rearrange(by_batch, j=J))
    feed_forward(nc, scratch.rearrange(by_batch, j=J), fc1_t, fc1_b, interp, fc2_t, fc2_b,
                 out.rearrange(by_batch, j=J))


def kernel(**inputs):
    import numpy as np
    import concourse.bacc as bacc
    from concourse.bass_utils import run_bass_kernel_spmd

    a = {k: np.ascontiguousarray(v) for k, v in inputs.items()}
    pos = np.arange(C, dtype=np.float32) / np.float32(C - 1) * np.float32(M2 - 1)
    at = np.clip(np.floor(pos).astype(np.int32), 0, M2 - 2)
    frac = (pos - at.astype(np.float32)).astype(np.float32)
    interp = np.zeros((C, M2), np.float32)
    interp[np.arange(C), at] = np.float32(1.0) - frac
    interp[np.arange(C), at + 1] = frac

    def tiles(w):
        return np.ascontiguousarray(w.reshape(-1, P, w.shape[1]).transpose(1, 0, 2))

    def by_tile(w, j):
        return np.ascontiguousarray(w.reshape(w.shape[0], P, j).transpose(0, 2, 1).reshape(w.shape[0], -1))

    arrays = {
        "x": a["x"].reshape(B, C, N),
        "wqkv_t": np.ascontiguousarray(a["L0_conv_w_qkv"].T).reshape(P, J * 3 * C),
        "wproj_t": tiles(by_tile(np.ascontiguousarray(a["L0_conv_w_proj"].T), J)).reshape(P, PAIRS * C),
        "bproj": a["L0_conv_b_proj"].reshape(P, J),
        "fc1_t": tiles(np.ascontiguousarray(a["L0_ffn_fc1_w"].T)),
        "fc1_b": np.ascontiguousarray(a["L0_ffn_fc1_b"].reshape(G, P).T),
        "interp": tiles(by_tile(interp, MT)),
        "fc2_t": tiles(by_tile(np.ascontiguousarray(a["L0_ffn_fc2_w"].T), MT)),
        "fc2_b": a["L0_ffn_fc2_b"].reshape(P, MT),
    }
    nc = bacc.Bacc("TRN2", target_bir_lowering=False, num_devices=1)
    aps = [nc.dram_tensor(f"in_{k}", v.shape, F32, kind="ExternalInput").ap() for k, v in arrays.items()]
    scratch = nc.dram_tensor("x1_scratch", (B, C, N), F32, kind="Internal").ap()
    out = nc.dram_tensor("out_0_dram", (B, C, N), F32, kind="ExternalOutput").ap()
    program(nc, *aps, scratch, out)
    r = run_bass_kernel_spmd(nc, [{f"in_{k}": v for k, v in arrays.items()}], core_ids=[0])
    return r.results[0]["out_0_dram"].reshape(B, C, 32, 32)
```

```python
from contextlib import ExitStack

import concourse.bass as bass
from concourse import mybir

F32 = mybir.dt.float32
F32R = mybir.dt.float32r
F16 = mybir.dt.float16
I32 = mybir.dt.int32
ALU = mybir.AluOpType
ACT = mybir.ActivationFunctionType
AX = mybir.AxisListType
RMAX = bass.bass_isa.ReduceOp.max

P = 128
B = 16
C = 512
J = C // P
N = 1024
H = N // 2
HD = 64
HEADS = C // HD
PAIRS = HEADS // 2
CHUNKS = N // P
HID = 2048
G = HID // P
M2 = C // 2
MT = M2 // P
T2 = N // 2
LN_C_EPS = 1e-6
LN_T_EPS = 1e-5

X_SCALE = 1024.0
E_SCALE = 32768.0
V_SCALE = 2.0 ** -19


MEAN_A = (1, 3)
CENTRE_A = (2, 4)
SQ_SUM_A = (2, 4)
VAR_A = (4, 6)
GUESS_A = (5, 7)

MEAN_PE = (4, 6)
VAR_PE = (9, 10)
CENTRE_AT = (3, 5)
SQUARE_AT = (4, 6)
GUESS_AT = 10
NEWTON_AT = 10
GAIN_AT = 12
BAND_AT = (11, 13)
RESULT_AT = (3, 4, 6, 7)


class Count:

    def __init__(self, sem, per, primed=False):
        self.sem, self.per, self.primed = sem, per, primed

    def at(self, b, n):
        return (b + (1 if self.primed else 0)) * self.per + n


def wait(eng, count, b, n):
    eng.wait_ge(count.sem, count.at(b, n))


class Norm:

    def __init__(self, nc, ctx, tag, eps, bank, ones, work=None):
        def sb(name, shape, dt=F32):
            return ctx.enter_context(nc.sbuf_tensor(f"{name}_{tag}", shape, dt))

        def cnt(name, per):
            return Count(ctx.enter_context(nc.semaphore(f"{name}_{tag}")), per)

        self.nc, self.eps, self.bank, self.ones = nc, eps, bank, ones
        self.banks = bank.shape[1]
        self.units = 2 // self.banks
        self.pair_sum = sb("pair_sum", [P, 2, H])
        self.sq = sb("sq", [P, J, H])
        self.total = sb("total", [P, H])
        self.sum_hi = sb("sum_hi", [P, 2, H], F32R)
        self.sum_lo = sb("sum_lo", [P, 2, H], F32R)
        self.eps_col = sb("eps_col", [P, 1])
        self.r0, self.m2r = work or (sb("r0", [P, N]), sb("m2r", [P, N]))
        self.x_pair = cnt("x_pair", 2)
        self.x_total = cnt("x_total", 2)
        self.x_summed = cnt("x_summed", 2)
        self.mean = cnt("mean", 2)
        self.centred = cnt("centred", 2)
        self.squared = cnt("squared", 2)
        self.sq_pair = cnt("sq_pair", 2)
        self.sq_total = cnt("sq_total", 2)
        self.sq_summed = cnt("sq_summed", 2)
        self.var = cnt("var", 2)
        self.logged = cnt("logged", self.units)
        self.guessed = cnt("guessed", self.units)
        self.guess_sq = cnt("guess_sq", self.units)
        self.guess_err = cnt("guess_err", self.units)
        self.inv_dev = cnt("inv_dev", self.units)

    def half_bank(self, h):
        return self.bank[:, h % self.banks, :]

    def unit_bank(self):
        return self.bank[:, :, :].rearrange("p a n -> p (a n)")

    def pool_parts(self, pool, b, h, totalled, summed):
        add, a, c = self.nc.gpsimd.tensor_tensor, self.pair_sum[:, 0, :], self.pair_sum[:, 1, :]
        add(self.total[:, :], a, c, ALU.add)
        add(self.sum_hi[:, h, :], a, c, ALU.add).then_inc(totalled.sem, 1)
        wait(pool, totalled, b, h + 1)
        add(self.sum_lo[:, h, :], self.total[:, :], self.sum_hi[:, h, :].bitcast(F32),
            ALU.subtract).then_inc(summed.sem, 1)

    def pool_sum(self, pool, x, b, h):
        t = slice(h * H, h * H + H)
        if h:
            wait(pool, self.x_summed, b, h)
        elif not (isinstance(b, int) and b == 0):
            wait(pool, self.sq_summed, b - 1, 2)
            wait(pool, self.var, b - 1, 2)
        self.nc.gpsimd.tensor_tensor(self.pair_sum[:, :, :], x[:, 0:2, t], x[:, 2:4, t],
                                     ALU.add).then_inc(self.x_pair.sem, 1)
        wait(pool, self.x_pair, b, h + 1)
        self.pool_parts(pool, b, h, self.x_total, self.x_summed)

    def pe_sum(self, h):
        self.nc.tensor.matmul(self.half_bank(h), self.ones[:, :], self.sum_hi[:, h, :], start=True, stop=False)
        return self.nc.tensor.matmul(self.half_bank(h), self.ones[:, :], self.sum_lo[:, h, :], start=False,
                                     stop=True)

    def pe_mean(self, pe, b, h):
        wait(pe, self.x_summed, b, h + 1)
        if h and self.banks == 1:
            wait(pe, self.centred, b, h)
        elif not (isinstance(b, int) and b == 0):
            wait(pe, self.guess_err, b - 1, self.units)
        self.pe_sum(h).then_inc(self.mean.sem, 1)

    def dve_centre(self, dve, x, out, b, h):
        t = slice(h * H, h * H + H)
        wait(dve, self.mean, b, h + 1)
        self.nc.vector.tensor_tensor(out[:, :, t], x[:, :, t],
                                     self.half_bank(h).unsqueeze(1).broadcast_to((P, J, H)),
                                     ALU.subtract).then_inc(self.centred.sem, 1)

    def act_square(self, act, xc, b, h):
        t = slice(h * H, h * H + H)
        wait(act, self.centred, b, h + 1)
        if h:
            wait(act, self.sq_pair, b, h)
        self.nc.scalar.activation(self.sq[:, :, :], xc[:, :, t], ACT.Square).then_inc(self.squared.sem, 1)

    def pool_sq_sum(self, pool, b, h):
        wait(pool, self.squared, b, h + 1)
        if h:
            wait(pool, self.sq_summed, b, h)
        else:
            wait(pool, self.x_summed, b, 2)
        self.nc.gpsimd.tensor_tensor(self.pair_sum[:, :, :], self.sq[:, 0:2, :], self.sq[:, 2:4, :],
                                     ALU.add).then_inc(self.sq_pair.sem, 1)
        wait(pool, self.sq_pair, b, h + 1)
        self.pool_parts(pool, b, h, self.sq_total, self.sq_summed)

    def pe_var(self, pe, b, h):
        wait(pe, self.sq_summed, b, h + 1)
        if self.banks == 2:
            wait(pe, self.centred, b, h + 1)
        elif h:
            wait(pe, self.guess_err, b, h)
        else:
            wait(pe, self.centred, b, 2)
        self.pe_sum(h).then_inc(self.var.sem, 1)

    def act_guess(self, act, b, u):
        if self.units == 1:
            self.nc.scalar.preload_act_table_set("natural_log_exp_and_others")
        wait(act, self.var, b, 2 if self.units == 1 else u + 1)
        if u:
            wait(act, self.inv_dev, b, u)
        self.nc.scalar.activation(self.r0[:, :], self.unit_bank(), ACT.Ln,
                                  bias=self.eps_col[:, 0:1]).then_inc(self.logged.sem, 1)
        wait(act, self.logged, b, u + 1)
        self.nc.scalar.activation(self.r0[:, :], self.r0[:, :], ACT.Exp,
                                  scale=-0.5).then_inc(self.guessed.sem, 1)

    def dve_newton(self, dve, b, u):
        nc = self.nc
        wait(dve, self.guessed, b, u + 1)
        nc.vector.tensor_tensor(self.m2r[:, :], self.r0[:, :], self.r0[:, :],
                                ALU.mult).then_inc(self.guess_sq.sem, 1)
        wait(dve, self.guess_sq, b, u + 1)
        nc.vector.scalar_tensor_tensor(self.m2r[:, :], self.unit_bank(), self.eps, self.m2r[:, :],
                                       ALU.add, ALU.mult).then_inc(self.guess_err.sem, 1)
        wait(dve, self.guess_err, b, u + 1)
        nc.vector.scalar_tensor_tensor(self.m2r[:, :], self.m2r[:, :], 3.0, self.r0[:, :],
                                       ALU.subtract, ALU.mult).then_inc(self.inv_dev.sem, 1)


def split3(nc, out, a_hi, a_lo, b_hi, b_lo, start, stop, skip=False):
    nc.tensor.matmul(out, a_hi, b_hi, start=start, stop=False, skip_group_check=skip)
    nc.tensor.matmul(out, a_hi, b_lo, start=False, stop=False, skip_group_check=skip)
    return nc.tensor.matmul(out, a_lo, b_hi, start=False, stop=stop, skip_group_check=skip)


def attention(nc, xb, xc, spare, handed, x1_stored, x_dram, wqkv_dram, wproj_dram, bproj_dram, x1_dram,
              fc1t_dram, interp_dram):
    ctx = ExitStack()
    with ctx:
        def sb(name, shape, dt=F32):
            return ctx.enter_context(nc.sbuf_tensor(name, shape, dt))

        def sem(name):
            return ctx.enter_context(nc.semaphore(name))

        def cnt(name, per, primed=False):
            return Count(sem(name), per, primed)

        wq_hi = sb("wq_hi", [P, J, 3 * C], F16)
        wq_lo = sb("wq_lo", [P, J, 3 * C], F16)
        wp_hi = sb("wp_hi", [P, PAIRS, C], F32R)
        wp_lo = sb("wp_lo", [P, PAIRS, C], F32R)
        xn_hi = sb("xn_hi", [P, J, N], F16)
        xn_lo = sb("xn_lo", [P, J, N], F16)
        e_tmp = sb("e_tmp", [P, 2, N])
        ek_hi = sb("ek_hi", [P, PAIRS, N], F32R)
        ek_lo = sb("ek_lo", [P, PAIRS, N], F32R)
        eq = sb("eq", [P, 2, C])
        vn = sb("vn", [P, 2, C])
        qk_st = xb[:, 1, :, :]
        v_st = e_tmp[:, :, :].rearrange("p a n -> p (a n)").rearrange("p (j n) -> p j n", j=J)
        wp_st = [eq, vn]
        eq_hi = sb("eq_hi", [P, 2, C], F16)
        eq_lo = sb("eq_lo", [P, 2, C], F16)
        vn_hi = sb("vn_hi", [P, 2, C], F16)
        vn_lo = sb("vn_lo", [P, 2, C], F16)
        qv_hi = sb("qv_hi", [P, PAIRS, P], F32R)
        qv_lo = sb("qv_lo", [P, PAIRS, P], F32R)
        mt_hi = sb("mt_hi", [P, PAIRS, C], F32R)
        mt_lo = sb("mt_lo", [P, PAIRS, C], F32R)
        ones = sb("ones", [P, P], F32R)
        bproj = sb("bproj", [P, J])
        small = sb("small", [P, 8])
        part_max = sb("part_max", [P, 2])
        row_max, all_max, exp_bits = small[:, 0:1], small[:, 1:2], small[:, 2:3]
        w_scale, un_scale, m_scale = small[:, 3:4], small[:, 4:5], small[:, 5:6]
        k_max = sb("k_max", [P, PAIRS])
        k_bias = sb("k_bias", [P, PAIRS])
        k_sum = sb("k_sum", [P, PAIRS])
        k_inv = sb("k_inv", [P, PAIRS])
        k_gain = sb("k_gain", [P, PAIRS])
        q_max = sb("q_max", [P, 2, HEADS])
        q_sum = sb("q_sum", [P, 2, HEADS])
        q_inv = sb("q_inv", [P, 2, HEADS])

        ring = [ctx.enter_context(nc.psum_tensor(f"ring{i}", [P, 2, H], F32)) for i in range(3)]
        qv_bank = ctx.enter_context(nc.psum_tensor("qv_bank", [P, PAIRS, P], F32))
        nbank = ctx.enter_context(nc.psum_tensor("norm_bank", [P, 1, H], F32))
        norm = Norm(nc, ctx, "a", LN_C_EPS, nbank, ones, (spare[:, 0:H], spare[:, H:N]))

        w_in = sem("w_in")
        v_in = sem("v_in")
        prep = sem("prep")
        wp_in = sem("wp_in")
        w_hi_done = sem("w_hi_done")
        w_lo_done = sem("w_lo_done")
        consts = sem("consts")
        maxed = sem("maxed")
        xl = cnt("x_loaded", 16)
        xs = cnt("x_scaled", 2)
        xhi = cnt("xn_hi_ready", 2)
        xlo = cnt("xn_lo_ready", 2)
        k_full = cnt("k_full", PAIRS)
        k_maxed = cnt("k_maxed", PAIRS)
        k_biased = cnt("k_biased", PAIRS)
        k_exp = cnt("k_exp", PAIRS)
        ek_hi_r = cnt("ek_hi_ready", PAIRS)
        ek_lo_r = cnt("ek_lo_ready", PAIRS - 1, True)
        q_full = cnt("q_full", CHUNKS)
        v_full = cnt("v_full", CHUNKS)
        q_maxed = cnt("q_maxed", CHUNKS)
        q_shift = cnt("q_shifted", CHUNKS)
        q_exp = cnt("q_exp", CHUNKS)
        q_summed = cnt("q_summed", CHUNKS)
        q_inved = cnt("q_inverted", CHUNKS)
        v_norm = cnt("v_normed", CHUNKS)
        eq_hi_r = cnt("eq_hi_ready", CHUNKS)
        eq_lo_r = cnt("eq_lo_ready", CHUNKS)
        vn_hi_r = cnt("vn_hi_ready", CHUNKS)
        vn_lo_r = cnt("vn_lo_ready", CHUNKS, True)
        qv_used = cnt("qv_used", CHUNKS, True)
        qv_hi_r = cnt("qv_hi_ready", 2)
        qv_lo_r = cnt("qv_lo_ready", 2, True)
        k_inved = cnt("k_inverted", 2)
        k_gained = cnt("k_gain_ready", 2)
        ek_last = cnt("ek_last_ready", 1, True)
        m_full = cnt("m_full", PAIRS)
        mt_hi_r = cnt("mt_hi_ready", PAIRS)
        mt_lo_r = cnt("mt_lo_ready", PAIRS)
        o_full = cnt("o_full", J, True)
        x1_r = cnt("x1_ready", J, True)

        block = ctx.enter_context(nc.Block())

        def batches(eng, body):
            with eng.Fori(0, B // 2 - 1) as i:
                for par in range(2):
                    body(i * 2 + par, par, False)
            for par in range(2):
                body(B - 2 + par, par, True)

        @block.sync
        def _(sp):
            sp.dma_start(xb[:, 0, :, :], x_dram[0]).then_inc(xl.sem, 16)
            sp.dma_start(qk_st, wqkv_dram[:, :, 0:2 * C]).then_inc(w_in, 16)
            sp.dma_start(v_st, wqkv_dram[:, :, 2 * C:3 * C]).then_inc(v_in, 16)
            for k in range(2):
                sp.dma_start(wp_st[k][:, :, :], wproj_dram[:, 2 * k:2 * k + 2, :]).then_inc(wp_in, 16)
            sp.dma_start(bproj[:, :], bproj_dram).then_inc(wp_in, 16)
            sp.wait_ge(w_lo_done, 3)
            wait(sp, xl, 0, 16)
            sp.dma_start(xb[:, 1, :, :], x_dram[1]).then_inc(xl.sem, 16)

            def body(b, par, last):
                for half in range(2):
                    j = slice(2 * half, 2 * half + 2)
                    wait(sp, x1_r, b, 2 * half + 2)
                    sp.dma_start(x1_dram[b][:, j, :], xb[:, par, j, :]).then_inc(x1_stored.sem, 16)
                if not (last and par):
                    wait(sp, x1_stored, b, 32)
                if not last:
                    sp.dma_start(xb[:, par, :, :], x_dram[b + 2]).then_inc(xl.sem, 16)
                elif par == 0:
                    sp.dma_start(xb[:, 0, :, :], fc1t_dram[:, :, 0:HID // 2]).then_inc(handed, 16)
                    wait(sp, xlo, b + 1, 2)
                    sp.dma_start(xc[:, :, :], x1_dram[0]).then_inc(handed, 16)
                    wait(sp, xs, b + 1, 2)
                    sp.dma_start(spare[:, :], interp_dram.rearrange("p j m -> p (j m)")).then_inc(handed, 16)

            batches(sp, body)

        @block.gpsimd
        def _(pool):
            nc.gpsimd.memset(ones[:, :].bitcast(F32), 1.0 / C).then_inc(consts, 1)
            nc.gpsimd.memset(norm.eps_col[:, :], LN_C_EPS).then_inc(consts, 1)
            nc.gpsimd.memset(qv_hi[:, :, :].bitcast(F32), 0.0).then_inc(consts, 1)
            nc.gpsimd.memset(qv_lo[:, :, :].bitcast(F32), 0.0).then_inc(consts, 1)
            pool.sem_inc(ek_lo_r.sem, PAIRS - 1)
            pool.sem_inc(vn_lo_r.sem, CHUNKS)

            def norm_sum(b, par, h):
                if h == 0:
                    wait(pool, xl, b, 16)
                norm.pool_sum(pool, xb[:, par, :, :], b, h)

            def xn_low(b, h):
                t = slice(h * H, h * H + H)
                wait(pool, xhi, b, h + 1)
                nc.gpsimd.tensor_tensor(xn_lo[:, :, t], xc[:, :, t], xn_hi[:, :, t],
                                        ALU.subtract).then_inc(xlo.sem, 1)

            def k_low(b, j):
                wait(pool, ek_hi_r, b, j + 1)
                nc.gpsimd.tensor_tensor(ek_lo[:, j, :], e_tmp[:, j % 2, :], ek_hi[:, j, :].bitcast(F32),
                                        ALU.subtract).then_inc(ek_lo_r.sem, 1)

            def v_low(b, t):
                wait(pool, vn_hi_r, b, t + 1)
                nc.gpsimd.tensor_tensor(vn_lo[:, t % 2, :], vn[:, t % 2, :], vn_hi[:, t % 2, :],
                                        ALU.subtract).then_inc(vn_lo_r.sem, 1)

            for h in range(2):
                norm_sum(0, 0, h)
            pool.wait_ge(prep, 1)
            nc.gpsimd.partition_all_reduce(all_max, row_max, P, RMAX).then_inc(prep, 1)
            for h in range(2):
                norm.pool_sq_sum(pool, 0, h)
            xn_low(0, 0)

            def body(b, par, last):
                more = not (last and par)
                k_low(b, 0)
                if more:
                    norm_sum(b + 1, 1 - par, 0)
                k_low(b, 1)
                for t in range(1, CHUNKS):
                    v_low(b, t - 1)
                    if more and t == 1:
                        norm_sum(b + 1, 1 - par, 1)
                    if more and t in SQ_SUM_A:
                        norm.pool_sq_sum(pool, b + 1, SQ_SUM_A.index(t))
                v_low(b, CHUNKS - 1)
                k_low(b, 2)
                if more:
                    for h in range(2):
                        xn_low(b + 1, h)

            batches(pool, body)

        @block.scalar
        def _(act):
            nc.scalar.preload_act_table_set("natural_log_exp_and_others")
            act.wait_ge(consts, 4)

            def qkv_high(part, staged):
                nc.scalar.activation(wq_hi[:, :, part * C:part * C + C], staged, ACT.Copy,
                                     scale=w_scale).then_inc(w_hi_done, 1)

            def xn_high(b, h, free):
                t = slice(h * H, h * H + H)
                wait(act, xs, b, h + 1)
                if free is not None:
                    wait(act, k_full, free, PAIRS)
                nc.scalar.activation(xn_hi[:, :, t], xc[:, :, t], ACT.Copy).then_inc(xhi.sem, 1)

            def k_tile(b, j, s):
                wait(act, k_biased, b, j + 1)
                if j == 0:
                    wait(act, ek_lo_r, b - 1, 3)
                elif j == 1:
                    wait(act, ek_last, b - 1, 1)
                else:
                    wait(act, ek_lo_r, b, j - 1)
                nc.scalar.activation(e_tmp[:, j % 2, :], ring[s % 3][:, :, :].rearrange("p a n -> p (a n)"),
                                     ACT.Exp, bias=k_bias[:, j:j + 1], scale=un_scale,
                                     accum_out=k_sum[:, j:j + 1]).then_inc(k_exp.sem, 1)

            def k_high(b, j):
                wait(act, k_exp, b, j + 1)
                wait(act, o_full, b - 1, J)
                nc.scalar.activation(ek_hi[:, j, :], e_tmp[:, j % 2, :], ACT.Copy).then_inc(ek_hi_r.sem, 1)

            def q_high(b, t):
                wait(act, q_shift, b, t + 1)
                nc.scalar.activation(eq[:, t % 2, :], eq[:, t % 2, :], ACT.Exp,
                                     scale=un_scale).then_inc(q_exp.sem, 1)
                wait(act, q_exp, b, t + 1)
                if t < 2:
                    wait(act, qv_used, b - 1, t + 7)
                else:
                    wait(act, qv_used, b, t - 1)
                nc.scalar.activation(eq_hi[:, t % 2, :], eq[:, t % 2, :], ACT.Copy,
                                     scale=E_SCALE).then_inc(eq_hi_r.sem, 1)

            def v_high(b, t):
                wait(act, v_norm, b, t + 1)
                nc.scalar.activation(vn_hi[:, t % 2, :], vn[:, t % 2, :], ACT.Copy).then_inc(vn_hi_r.sem, 1)

            norm.act_square(act, xc, 0, 0)
            act.wait_ge(prep, 6)
            qkv_high(1, qk_st[:, :, C:2 * C])
            norm.act_square(act, xc, 0, 1)
            qkv_high(0, qk_st[:, :, 0:C])
            qkv_high(2, v_st)
            for h in range(2):
                norm.act_guess(act, 0, h)
                xn_high(0, h, None)
            act.wait_ge(wp_in, 48)
            for k in range(2):
                nc.scalar.activation(wp_hi[:, 2 * k:2 * k + 2, :], wp_st[k][:, :, :],
                                     ACT.Copy).then_inc(w_hi_done, 1)

            def body(b, par, last):
                more = not (last and par)
                for j in range(2):
                    k_tile(b, j, j)
                    k_high(b, j)
                for t in range(CHUNKS):
                    if more and t in CENTRE_A:
                        norm.act_square(act, xc, b + 1, CENTRE_A.index(t))
                    if more and t in GUESS_A:
                        norm.act_guess(act, b + 1, GUESS_A.index(t))
                    q_high(b, t)
                    if t:
                        v_high(b, t - 1)
                v_high(b, CHUNKS - 1)
                k_tile(b, 2, 10)
                k_high(b, 2)
                wait(act, qv_used, b, CHUNKS)
                for d in range(2):
                    s = slice(d * HD, d * HD + HD)
                    nc.scalar.activation(qv_hi[s, :, s], qv_bank[s, :, s], ACT.Copy).then_inc(qv_hi_r.sem, 1)
                for p in range(PAIRS):
                    if p == 2:
                        k_tile(b, 3, 11)
                    if p == 3:
                        k_high(b, 3)
                    wait(act, m_full, b, p + 1)
                    if p in (0, 3):
                        wait(act, k_gained, b, 1 + p // 3)
                    nc.scalar.activation(mt_hi[:, p, :], ring[(12 + p // 2) % 3][:, p % 2, :], ACT.Copy,
                                         scale=k_gain[:, p:p + 1]).then_inc(mt_hi_r.sem, 1)
                if more:
                    for h in range(2):
                        xn_high(b + 1, h, b)

            batches(act, body)

        @block.vector
        def _(dve):
            dve.sem_inc(x1_r.sem, J)
            dve.sem_inc(ek_last.sem, 1)
            dve.sem_inc(qv_lo_r.sem, 2)

            def weight_scales():
                for k, (staged, loaded) in enumerate(((qk_st, w_in), (v_st, v_in))):
                    dve.wait_ge(loaded, 16)
                    nc.vector.tensor_reduce(part_max[:, k:k + 1], staged, AX.XY, ALU.max,
                                            apply_absolute_value=True).then_inc(maxed, 1)
                dve.wait_ge(maxed, 2)
                nc.vector.tensor_reduce(row_max, part_max[:, :], AX.X, ALU.max).then_inc(prep, 1)

            def weight_scales_after_pool():
                dve.wait_ge(prep, 2)
                nc.vector.tensor_scalar_max(exp_bits, all_max, 1e-30).then_inc(prep, 1)
                dve.wait_ge(prep, 3)
                nc.vector.tensor_scalar(exp_bits.bitcast(I32), exp_bits.bitcast(I32), 0x7F800000, None,
                                        ALU.bitwise_and).then_inc(prep, 1)
                dve.wait_ge(prep, 4)
                nc.vector.tensor_scalar(un_scale.bitcast(I32), exp_bits.bitcast(I32), 1.0,
                                        float(-24 * 2 ** 23), ALU.mult, ALU.add)
                nc.vector.tensor_scalar(m_scale.bitcast(I32), exp_bits.bitcast(I32), 1.0,
                                        float(-20 * 2 ** 23), ALU.mult, ALU.add).then_inc(prep, 1)
                nc.vector.tensor_scalar(w_scale.bitcast(I32), exp_bits.bitcast(I32), -1.0,
                                        float(268 * 2 ** 23), ALU.mult, ALU.add).then_inc(prep, 1)
                dve.wait_ge(prep, 6)

            def qkv_low(n, part, staged):
                dve.wait_ge(w_hi_done, n)
                w = slice(part * C, part * C + C)
                nc.vector.scalar_tensor_tensor(wq_lo[:, :, w], staged, w_scale, wq_hi[:, :, w], ALU.mult,
                                               ALU.subtract).then_inc(w_lo_done, 1)

            def projection_low():
                for k in range(2):
                    p = slice(2 * k, 2 * k + 2)
                    dve.wait_ge(w_hi_done, 4 + k)
                    nc.vector.tensor_tensor(wp_lo[:, p, :], wp_st[k][:, :, :], wp_hi[:, p, :].bitcast(F32),
                                            ALU.subtract).then_inc(w_lo_done, 1)

            def newton(b, h):
                if h:
                    wait(dve, xs, b, h)
                elif not (isinstance(b, int) and b == 0):
                    wait(dve, xs, b - 1, 2)
                norm.dve_newton(dve, b, h)

            def x_scale(b, h):
                t = slice(h * H, h * H + H)
                wait(dve, norm.inv_dev, b, h + 1)
                wait(dve, norm.squared, b, h + 1)
                nc.vector.scalar_tensor_tensor(
                    xc[:, :, t], xc[:, :, t], -0.5 * X_SCALE,
                    norm.m2r[:, :].unsqueeze(1).broadcast_to((P, J, H)), ALU.mult, ALU.mult).then_inc(xs.sem, 1)

            def centre(b, par, h):
                if h == 0:
                    wait(dve, xl, b, 16)
                norm.dve_centre(dve, xb[:, par, :, :], xc, b, h)

            def k_tile(b, j, s):
                wait(dve, k_full, b, j + 1)
                nc.vector.reduce_max(k_max[:, j:j + 1], ring[s % 3][:, :, :].rearrange("p a n -> p (a n)"),
                                     AX.X).then_inc(k_maxed.sem, 1)
                wait(dve, k_maxed, b, j + 1)
                nc.vector.tensor_scalar(k_bias[:, j:j + 1], k_max[:, j:j + 1], un_scale, -1.0, ALU.mult,
                                        ALU.mult).then_inc(k_biased.sem, 1)

            def heads(ap):
                return ap.rearrange("p (h d) -> p h d", h=HEADS)

            def spread(ap):
                return ap.unsqueeze(2).broadcast_to((P, HEADS, HD))

            def q_shift_chunk(b, t):
                bank = ring[(t + 2) % 3][:, 0, :]
                wait(dve, q_full, b, t + 1)
                nc.vector.reduce_max(q_max[:, t % 2, :], heads(bank), AX.X).then_inc(q_maxed.sem, 1)
                wait(dve, q_maxed, b, t + 1)
                if t >= 2:
                    wait(dve, eq_hi_r, b, t - 1)
                nc.vector.tensor_tensor(heads(eq[:, t % 2, :]), heads(bank), spread(q_max[:, t % 2, :]),
                                        ALU.subtract).then_inc(q_shift.sem, 1)

            def v_chunk(b, t):
                bank = ring[(t + 2) % 3][:, 1, :]
                wait(dve, q_exp, b, t + 1)
                nc.vector.reduce_sum(q_sum[:, t % 2, :], heads(eq[:, t % 2, :]), AX.X).then_inc(q_summed.sem, 1)
                wait(dve, q_summed, b, t + 1)
                nc.vector.reciprocal(q_inv[:, t % 2, :], q_sum[:, t % 2, :]).then_inc(q_inved.sem, 1)
                wait(dve, q_inved, b, t + 1)
                wait(dve, v_full, b, t + 1)
                if t >= 2:
                    wait(dve, vn_lo_r, b, t - 1)
                else:
                    wait(dve, vn_lo_r, b - 1, t + 7)
                nc.vector.scalar_tensor_tensor(heads(vn[:, t % 2, :]), heads(bank), V_SCALE,
                                               spread(q_inv[:, t % 2, :]), ALU.mult,
                                               ALU.mult).then_inc(v_norm.sem, 1)

            def q_low(b, t):
                wait(dve, eq_hi_r, b, t + 1)
                nc.vector.scalar_tensor_tensor(eq_lo[:, t % 2, :], eq[:, t % 2, :], E_SCALE,
                                               eq_hi[:, t % 2, :], ALU.mult,
                                               ALU.subtract).then_inc(eq_lo_r.sem, 1)

            weight_scales()
            centre(0, 0, 0)
            weight_scales_after_pool()
            centre(0, 0, 1)
            qkv_low(1, 1, qk_st[:, :, C:2 * C])
            qkv_low(2, 0, qk_st[:, :, 0:C])
            qkv_low(3, 2, v_st)
            for h in range(2):
                newton(0, h)
                x_scale(0, h)
            wait(dve, xhi, 0, 2)
            wait(dve, xlo, 0, 1)
            nc.vector.tensor_tensor(xn_lo[:, :, H:N], xc[:, :, H:N], xn_hi[:, :, H:N],
                                    ALU.subtract).then_inc(xlo.sem, 1)
            projection_low()

            def body(b, par, last):
                more = not (last and par)
                k_tile(b, 0, 0)
                k_tile(b, 1, 1)
                for t in range(CHUNKS):
                    if more and t in CENTRE_A:
                        if t == CENTRE_A[0]:
                            wait(dve, xlo, b, 2)
                        centre(b + 1, 1 - par, CENTRE_A.index(t))
                    q_shift_chunk(b, t)
                    if more and t in GUESS_A:
                        newton(b + 1, GUESS_A.index(t))
                    if t:
                        v_chunk(b, t - 1)
                        q_low(b, t - 1)
                    if more and t == 6:
                        x_scale(b + 1, 0)
                v_chunk(b, CHUNKS - 1)
                q_low(b, CHUNKS - 1)
                k_tile(b, 2, 10)
                if more:
                    x_scale(b + 1, 1)
                for d in range(2):
                    s = slice(d * HD, d * HD + HD)
                    wait(dve, qv_hi_r, b, 2)
                    nc.vector.tensor_tensor(qv_lo[s, :, s], qv_bank[s, :, s], qv_hi[s, :, s].bitcast(F32),
                                            ALU.subtract).then_inc(qv_lo_r.sem, 1)

                def k_gains(n, js):
                    wait(dve, k_exp, b, js.stop)
                    nc.vector.reciprocal(k_inv[:, js], k_sum[:, js]).then_inc(k_inved.sem, 1)
                    wait(dve, k_inved, b, n)
                    nc.vector.tensor_scalar(k_gain[:, js], k_inv[:, js], m_scale, None,
                                            ALU.mult).then_inc(k_gained.sem, 1)

                k_gains(1, slice(0, 3))
                k_tile(b, 3, 11)
                for p in range(PAIRS):
                    if p == 3:
                        k_gains(2, slice(3, 4))
                        wait(dve, ek_hi_r, b, PAIRS)
                        nc.vector.tensor_tensor(ek_lo[:, 3, :], e_tmp[:, 1, :], ek_hi[:, 3, :].bitcast(F32),
                                                ALU.subtract).then_inc(ek_last.sem, 1)
                    if p in (0, 3):
                        wait(dve, k_gained, b, 1 + p // 3)
                    wait(dve, mt_hi_r, b, p + 1)
                    nc.vector.scalar_tensor_tensor(mt_lo[:, p, :], ring[(12 + p // 2) % 3][:, p % 2, :],
                                                   k_gain[:, p:p + 1], mt_hi[:, p, :].bitcast(F32),
                                                   ALU.mult, ALU.subtract).then_inc(mt_lo_r.sem, 1)
                for j in range(J):
                    wait(dve, o_full, b, j + 1)
                    nc.vector.scalar_tensor_tensor(
                        xb[:, par, j, :], ring[(14 + j) % 3][:, :, :].rearrange("p a n -> p (a n)"),
                        bproj[:, j:j + 1], xb[:, par, j, :], ALU.add, ALU.add).then_inc(x1_r.sem, 1)

            batches(dve, body)

        @block.tensor
        def _(pe):
            pe.sem_inc(o_full.sem, J)
            pe.sem_inc(qv_used.sem, CHUNKS)
            pe.wait_ge(consts, 4)

            def k_half(b, j, s, h):
                t = slice(h * H, h * H + H)
                w = slice(C + j * P, C + j * P + P)
                for c in range(J):
                    last = split3(nc, ring[s % 3][:, h, :], wq_hi[:, c, w], wq_lo[:, c, w], xn_hi[:, c, t],
                                  xn_lo[:, c, t], c == 0, c == J - 1)
                return last

            def chunk(b, t):
                ts = slice(t * P, t * P + P)
                for part, count in ((0, q_full), (1, v_full)):
                    w = slice(part * 2 * C, part * 2 * C + C)
                    for c in range(J):
                        last = split3(nc, ring[(t + 2) % 3][:, part, :], xn_hi[:, c, ts], xn_lo[:, c, ts],
                                      wq_hi[:, c, w], wq_lo[:, c, w], c == 0, c == J - 1)
                    last.then_inc(count.sem, 1)

            def qv_chunk(b, t):
                wait(pe, eq_lo_r, b, t + 1)
                wait(pe, vn_lo_r, b, t + 1)
                if t == 0:
                    wait(pe, qv_lo_r, b - 1, 2)
                i = t % 2
                for p in range(PAIRS):
                    s = slice(p * P, p * P + P)
                    last = split3(nc, qv_bank[:, p, :], eq_hi[:, i, s], eq_lo[:, i, s], vn_hi[:, i, s],
                                  vn_lo[:, i, s], t == 0 and p == 0, t == CHUNKS - 1, True)
                last.then_inc(qv_used.sem, 1)

            for h in range(2):
                norm.pe_mean(pe, 0, h)
            for h in range(2):
                norm.pe_var(pe, 0, h)
            pe.wait_ge(w_lo_done, 3)

            def body(b, par, last):
                more = not (last and par)
                wait(pe, x1_r, b - 1, 2)
                for h in range(2):
                    wait(pe, xlo, b, h + 1)
                    k = k_half(b, 0, 0, h)
                k.then_inc(k_full.sem, 1)
                wait(pe, x1_r, b - 1, 3)
                for h in range(2):
                    k = k_half(b, 1, 1, h)
                k.then_inc(k_full.sem, 1)
                for t in range(CHUNKS):
                    if t == 0:
                        wait(pe, x1_r, b - 1, 4)
                    elif t < 3:
                        wait(pe, k_exp, b, t)
                    else:
                        wait(pe, v_norm, b, t - 2)
                    chunk(b, t)
                    if t >= 2:
                        qv_chunk(b, t - 2)
                    if more and t in MEAN_A:
                        norm.pe_mean(pe, b + 1, MEAN_A.index(t))
                    if more and t in VAR_A:
                        norm.pe_var(pe, b + 1, VAR_A.index(t))
                wait(pe, v_norm, b, 6)
                for h in range(2):
                    k = k_half(b, 2, 10, h)
                k.then_inc(k_full.sem, 1)
                qv_chunk(b, 6)
                wait(pe, v_norm, b, 7)
                k_half(b, 3, 11, 0)
                qv_chunk(b, 7)
                k_half(b, 3, 11, 1).then_inc(k_full.sem, 1)
                wait(pe, qv_lo_r, b, 2)
                pe.wait_ge(w_lo_done, 5)
                for p in range(PAIRS):
                    if p == 0:
                        wait(pe, v_norm, b, 8)
                    if p == 2:
                        wait(pe, k_exp, b, 3)
                    split3(nc, ring[(12 + p // 2) % 3][:, p % 2, :], qv_hi[:, p, :], qv_lo[:, p, :],
                           wp_hi[:, p, :], wp_lo[:, p, :], True, True).then_inc(m_full.sem, 1)
                for j in range(J):
                    if j == 0:
                        wait(pe, k_exp, b, 4)
                    elif j == 3:
                        wait(pe, x1_r, b, 1)
                    js = slice(j * P, j * P + P)
                    for p in range(PAIRS):
                        if j == 0:
                            wait(pe, mt_lo_r, b, p + 1)
                            if p < 3:
                                wait(pe, ek_lo_r, b, p + 1)
                            else:
                                wait(pe, ek_last, b, 1)
                        for h in range(2):
                            t = slice(h * H, h * H + H)
                            last = split3(nc, ring[(14 + j) % 3][:, h, :], mt_hi[:, p, js], mt_lo[:, p, js],
                                          ek_hi[:, p, t], ek_lo[:, p, t], p == 0, p == PAIRS - 1)
                    last.then_inc(o_full.sem, 1)

            batches(pe, body)


def feed_forward(nc, zb, xb, spare, handed, x1_stored, x1_dram, fc1t_dram, fc1b_dram, fc2t_dram, fc2b_dram, out_dram):
    ctx = ExitStack()
    with ctx:
        def sb(name, shape, dt=F32):
            return ctx.enter_context(nc.sbuf_tensor(name, shape, dt))

        def sem(name):
            return ctx.enter_context(nc.semaphore(name))

        def cnt(name, per, primed=False):
            return Count(sem(name), per, primed)

        LAG = 3
        HB = 4
        w1_hi = sb("w1_hi", [P, MT, HID], F32R)
        w1_lo = sb("w1_lo", [P, MT, HID], F32R)
        w2_hi = sb("w2_hi", [P, G, M2], F32R)
        w2_lo = sb("w2_lo", [P, G, M2], F32R)
        w1_st = [zb[:, k, :, :] for k in range(2)]
        w2_st = zb[:, 0, :, :].rearrange("p j n -> p (j n)").rearrange("p (g m) -> p g m", g=G)
        ones = sb("f_ones", [P, P], F32R)
        fc1b = sb("fc1b", [P, G])
        fc2b = sb("fc2b", [P, MT])
        mean = sb("mean_row", [P, 2, N])
        gain = sb("gain", [P, N])
        quad = sb("quad", [P, 2, MT, T2])
        ll_hi = sb("ll_hi", [P, MT, T2], F32R)
        ll_lo = sb("ll_lo", [P, MT, T2], F32R)
        ht_more = sb("ht_more", [P, 2, T2])
        ht = [spare[:, 0:T2], spare[:, T2:N], ht_more[:, 0, :], ht_more[:, 1, :]]
        h_hi = sb("h_hi", [P, 4, T2], F32R)
        h_lo = sb("h_lo", [P, 4, T2], F32R)
        change = sb("change", [P, MT, T2])
        add = sb("add", [P, MT, N])
        interp = spare[:, :].rearrange("p (j m) -> p j m", j=J)

        hbank = [ctx.enter_context(nc.psum_tensor(f"hbank{i}", [P, T2], F32)) for i in range(HB)]
        obank = ctx.enter_context(nc.psum_tensor("obank", [P, MT, T2], F32))
        nbank = ctx.enter_context(nc.psum_tensor("f_norm_bank", [P, 2, H], F32))
        norm = Norm(nc, ctx, "b", LN_T_EPS, nbank, ones)

        w_in = sem("f_w_in")
        w1b_in = sem("w1b_in")
        w2_in = sem("w2_in")
        consts = sem("f_consts")
        w1_full = sem("w1_full")
        w1_hi_r = sem("w1_hi_ready")
        w1_lo_r = sem("w1_lo_ready")
        w2_hi_r = sem("w2_hi_ready")
        w2_lo_r = sem("w2_lo_ready")
        xl = [cnt(f"f_x_loaded{h}", 16) for h in range(2)]
        meaned = cnt("mean_kept", 2)
        paired = cnt("channel_pairs", 2)
        pair_normed = cnt("pairs_normed", 2)
        quaded = cnt("quads", 2)
        ll_hi_r = cnt("ll_hi_ready", 1)
        ll_lo_r = cnt("ll_lo_ready", 1)
        gained = cnt("gain_ready", 1)
        scaled = [cnt("x_gained_pool", 2), cnt("x_gained_dve", 2)]
        h_full = cnt("h_full", G)
        h_act = cnt("h_gelu", G)
        h_hi_r = cnt("h_hi_ready", G)
        h_lo_r = cnt("h_lo_ready", G, True)
        h_used = cnt("h_used", G, True)
        changed = cnt("change_raw", MT)
        halved = cnt("change_ready", MT)
        added = cnt("add_ready", MT)
        z_r = cnt("z_ready", J)
        z_stored = [cnt(f"z_stored{par}", 16) for par in range(2)]

        block = ctx.enter_context(nc.Block())

        def batches(eng, body):
            for par in range(2):
                body(par, par, False, par == 0)
            with eng.Fori(1, B // 2 - 1) as i:
                for par in range(2):
                    body(i * 2 + par, par, False, False)
            for par in range(2):
                body(B - 2 + par, par, True, False)

        def z_free(eng, b, par):
            if isinstance(b, int) and b < 2:
                eng.wait_ge(w2_lo_r, 1)
            else:
                wait(eng, z_stored[par], b - par - 2, 32)

        @block.sync
        def _(sp):
            sp.dma_start(fc1b[:, :], fc1b_dram).then_inc(w_in, 16)
            sp.dma_start(fc2b[:, :], fc2b_dram).then_inc(w_in, 16)
            wait(sp, x1_stored, B - 1, 32)
            sp.dma_start(w1_st[1], fc1t_dram[:, :, HID // 2:HID]).then_inc(w1b_in, 16)
            sp.wait_ge(w1_full, 4)
            sp.dma_start(w2_st, fc2t_dram).then_inc(w2_in, 16)

            def store(b, par):
                for half in range(2):
                    j = slice(2 * half, 2 * half + 2)
                    wait(sp, z_r, b, 2 * half + 2)
                    sp.dma_start(out_dram[b][:, j, :], zb[:, par, j, :]).then_inc(z_stored[par].sem, 16)

            def body(b, par, last, first):
                if not (last and par):
                    for h in range(2):
                        t = slice(h * H, h * H + H)
                        for part in scaled:
                            wait(sp, part, b, h + 1)
                        sp.dma_start(xb[:, :, t], x1_dram[b + 1][:, :, t]).then_inc(xl[h].sem, 16)
                if not first:
                    store(b - 1, 1 - par)
                if last and par:
                    store(b, par)
                    for k in range(2):
                        wait(sp, z_stored[k], b - par, 32)

            batches(sp, body)

        @block.gpsimd
        def _(pool):
            nc.gpsimd.memset(ones[:, :].bitcast(F32), 1.0 / C).then_inc(consts, 1)
            nc.gpsimd.memset(norm.eps_col[:, :], LN_T_EPS).then_inc(consts, 1)

            def sums(b, par):
                for h in range(2):
                    if isinstance(b, int) and b == 0:
                        pool.wait_ge(handed, 48)
                    else:
                        wait(pool, xl[h], b - 1, 16)
                    norm.pool_sum(pool, xb, b, h)

            def pair(b, par, h):
                t = slice(h * H, h * H + H)
                wait(pool, norm.centred, b, h + 1)
                if not (isinstance(b, int) and b < 2):
                    wait(pool, z_r, b - 2, J)
                nc.gpsimd.tensor_tensor(add[:, :, t], xb[:, 0:4:2, t], xb[:, 1:4:2, t],
                                        ALU.add).then_inc(paired.sem, 1)

            def gains(b, par, h):
                t = slice(h * H, h * H + H)
                wait(pool, gained, b, 1)
                z_free(pool, b, par)
                nc.gpsimd.tensor_tensor(zb[:, par, 0:2, t], xb[:, 0:2, t],
                                        gain[:, t].unsqueeze(1).broadcast_to((P, 2, H)),
                                        ALU.mult).then_inc(scaled[0].sem, 1)

            def pre(b, par):
                sums(b, par)
                for h in range(2):
                    norm.pool_sq_sum(pool, b, h)
                for h in range(2):
                    pair(b, par, h)
                if isinstance(b, int) and b == 0:
                    pool.wait_ge(w2_hi_r, 1)
                    nc.gpsimd.tensor_tensor(w2_lo[:, :, :], w2_st, w2_hi[:, :, :].bitcast(F32),
                                            ALU.subtract).then_inc(w2_lo_r, 1)
                for h in range(2):
                    gains(b, par, h)

            pre(0, 0)

            def body(b, par, last, first):
                if not (last and par):
                    pre(b + 1, 1 - par)

            batches(pool, body)

        @block.scalar
        def _(act):
            act.wait_ge(consts, 2)

            def fc1_high(i):
                n, m = i // MT, i % MT
                act.wait_ge(w1_full, i + 1)
                nc.scalar.activation(w1_hi[:, m, n * H:n * H + H], hbank[i % HB][:, :],
                                     ACT.Copy).then_inc(w1_hi_r, 1)

            def keep_mean(b, par, h):
                wait(act, norm.centred, b, h + 1)
                nc.scalar.activation(mean[:, par, h * H:h * H + H], nbank[:, h, :], ACT.Copy).then_inc(meaned.sem, 1)

            def ll_high(b, par, free):
                wait(act, quaded, b, 2)
                if free is not None:
                    wait(act, h_full, free, G)
                nc.scalar.activation(ll_hi[:, :, :], quad[:, par, :, :], ACT.Copy,
                                     scale=-0.25).then_inc(ll_hi_r.sem, 1)

            def hidden(b, g):
                wait(act, h_full, b, g + 1)
                if g >= 4:
                    wait(act, h_lo_r, b, g - 3)
                else:
                    wait(act, h_lo_r, b - 1, G + g - 3)
                nc.scalar.activation(ht[g % 4], hbank[g % HB][:, :], ACT.Gelu,
                                     bias=fc1b[:, g:g + 1]).then_inc(h_act.sem, 1)
                wait(act, h_act, b, g + 1)
                if g >= 4:
                    wait(act, h_used, b, g - 3)
                else:
                    wait(act, h_used, b - 1, G + g - 3)
                nc.scalar.activation(h_hi[:, g % 4, :], ht[g % 4], ACT.Copy).then_inc(h_hi_r.sem, 1)

            fc1_high(0)
            fc1_high(1)
            for h in range(2):
                keep_mean(0, 0, h)
                norm.act_square(act, xb, 0, h)
                fc1_high(2 + h)
            fc1_high(4)
            act.wait_ge(w2_in, 16)
            nc.scalar.activation(w2_hi[:, :, :], w2_st, ACT.Copy).then_inc(w2_hi_r, 1)
            norm.act_guess(act, 0, 0)
            for i in range(5, 8):
                fc1_high(i)
            ll_high(0, 0, None)
            act.wait_ge(w_in, 32)

            def body(b, par, last, first):
                more = not (last and par)
                for g in range(G):
                    if more and g in SQUARE_AT:
                        h = SQUARE_AT.index(g)
                        keep_mean(b + 1, 1 - par, h)
                        norm.act_square(act, xb, b + 1, h)
                    if more and g == GUESS_AT:
                        norm.act_guess(act, b + 1, 0)
                    hidden(b, g)
                if more:
                    ll_high(b + 1, 1 - par, b)

            batches(act, body)

        @block.vector
        def _(dve):
            dve.sem_inc(h_lo_r.sem, G)

            def fc1_low(i):
                n, m = i // MT, i % MT
                dve.wait_ge(w1_hi_r, i + 1)
                nc.vector.tensor_tensor(w1_lo[:, m, n * H:n * H + H], hbank[i % HB][:, :],
                                        w1_hi[:, m, n * H:n * H + H].bitcast(F32),
                                        ALU.subtract).then_inc(w1_lo_r, 1)

            def centre(b, par, h):
                wait(dve, norm.x_pair, b, h + 1)
                norm.dve_centre(dve, xb, xb, b, h)

            def gain_row(b):
                wait(dve, norm.inv_dev, b, 1)
                nc.vector.tensor_scalar(gain[:, :], norm.m2r[:, :], -0.5, 1.0, ALU.mult,
                                        ALU.add).then_inc(gained.sem, 1)

            def low_band(b, par, h):
                t = slice(h * H, h * H + H)
                t2 = slice(h * H // 2, h * H // 2 + H // 2)
                wait(dve, norm.inv_dev, b, 1)
                wait(dve, paired, b, h + 1)
                nc.vector.tensor_tensor(add[:, :, t], add[:, :, t],
                                        norm.m2r[:, t].unsqueeze(1).broadcast_to((P, MT, H)),
                                        ALU.mult).then_inc(pair_normed.sem, 1)
                wait(dve, pair_normed, b, h + 1)
                nc.vector.tensor_tensor(quad[:, par, :, t2], add[:, :, h * H:h * H + H:2],
                                        add[:, :, h * H + 1:h * H + H:2],
                                        ALU.add).then_inc(quaded.sem, 1)

            def gains(b, par, h):
                t = slice(h * H, h * H + H)
                wait(dve, gained, b, 1)
                z_free(dve, b, par)
                nc.vector.tensor_tensor(zb[:, par, 2:4, t], xb[:, 2:4, t],
                                        gain[:, t].unsqueeze(1).broadcast_to((P, 2, H)),
                                        ALU.mult).then_inc(scaled[1].sem, 1)

            def ll_low(b, par):
                wait(dve, ll_hi_r, b, 1)
                wait(dve, quaded, b, 2)
                nc.vector.scalar_tensor_tensor(ll_lo[:, :, :], quad[:, par, :, :], -0.25,
                                               ll_hi[:, :, :].bitcast(F32), ALU.mult,
                                               ALU.subtract).then_inc(ll_lo_r.sem, 1)

            def hidden_low(b, g):
                wait(dve, h_hi_r, b, g + 1)
                nc.vector.tensor_tensor(h_lo[:, g % 4, :], ht[g % 4], h_hi[:, g % 4, :].bitcast(F32),
                                        ALU.subtract).then_inc(h_lo_r.sem, 1)

            def result_change(b, par):
                wait(dve, h_used, b, G)
                for m in range(MT):
                    nc.vector.scalar_tensor_tensor(change[:, m, :], quad[:, par, m, :], 0.25,
                                                   obank[:, m, :], ALU.mult,
                                                   ALU.add).then_inc(changed.sem, 1)
                for m in range(MT):
                    wait(dve, changed, b, m + 1)
                    nc.vector.tensor_scalar(change[:, m, :], change[:, m, :], fc2b[:, m:m + 1], 0.5,
                                            ALU.add, ALU.mult).then_inc(halved.sem, 1)

            def result_add(b, par):
                wait(dve, meaned, b, 2)
                for m in range(MT):
                    wait(dve, halved, b, m + 1)
                    nc.vector.tensor_tensor(add[:, m, :].rearrange("p (t s) -> p t s", s=2),
                                            change[:, m, :].unsqueeze(2).broadcast_to((P, T2, 2)),
                                            mean[:, par, :].rearrange("p (t s) -> p t s", s=2),
                                            ALU.add).then_inc(added.sem, 1)

            def result(b, par, j):
                wait(dve, added, b, j // 2 + 1)
                wait(dve, scaled[j // 2], b, 2)
                nc.vector.tensor_tensor(zb[:, par, j, :], zb[:, par, j, :], add[:, j // 2, :],
                                        ALU.add).then_inc(z_r.sem, 1)

            for h in range(2):
                fc1_low(h)
                centre(0, 0, h)
            for i in range(2, 5):
                fc1_low(i)
            norm.dve_newton(dve, 0, 0)
            gain_row(0)
            for h in range(2):
                low_band(0, 0, h)
            for i in range(5, 8):
                fc1_low(i)
            ll_low(0, 0)
            for h in range(2):
                gains(0, 0, h)
            dve.wait_ge(w_in, 32)

            def body(b, par, last, first):
                more = not (last and par)
                for g in range(G):
                    if not first and g == 0:
                        result_change(b - 1, 1 - par)
                    if not first and g == 1:
                        result_add(b - 1, 1 - par)
                    if more and g in CENTRE_AT:
                        centre(b + 1, 1 - par, CENTRE_AT.index(g))
                    for j in range(J):
                        if not first and g == RESULT_AT[j]:
                            result(b - 1, 1 - par, j)
                    if more and g == NEWTON_AT:
                        norm.dve_newton(dve, b + 1, 0)
                        gain_row(b + 1)
                    if more and g == GAIN_AT:
                        gains(b + 1, 1 - par, 0)
                    if more and g in BAND_AT:
                        low_band(b + 1, 1 - par, BAND_AT.index(g))
                    hidden_low(b, g)
                if more:
                    ll_low(b + 1, 1 - par)
                    gains(b + 1, 1 - par, 1)
                else:
                    result_change(b, par)
                    result_add(b, par)
                    for j in range(J):
                        result(b, par, j)

            batches(dve, body)

        @block.tensor
        def _(pe):
            pe.sem_inc(h_used.sem, G)
            pe.wait_ge(consts, 2)
            pe.wait_ge(handed, 48)
            for i in range(MT * 4):
                n, m = i // MT, i % MT
                if i == 4:
                    pe.wait_ge(w1b_in, 16)
                if i >= HB:
                    pe.wait_ge(w1_lo_r, i - HB + 1)
                for c in range(J):
                    last = nc.tensor.matmul(hbank[i % HB][:, :], interp[:, c, m * P:m * P + P],
                                            w1_st[n // 2][:, c, n % 2 * H:n % 2 * H + H], start=c == 0,
                                            stop=c == J - 1)
                last.then_inc(w1_full, 1)
                if i in (1, 2):
                    norm.pe_mean(pe, 0, i - 1)
                if i == 4:
                    wait(pe, meaned, 0, 2)
                if i in (4, 5):
                    norm.pe_var(pe, 0, i - 4)
            pe.wait_ge(w1_lo_r, MT * 4)

            def fc1(b, g):
                if g >= HB:
                    wait(pe, h_act, b, g - HB + 1)
                gs = slice(g * P, g * P + P)
                for m in range(MT):
                    last = split3(nc, hbank[g % HB][:, :], w1_hi[:, m, gs], w1_lo[:, m, gs], ll_hi[:, m, :],
                                  ll_lo[:, m, :], m == 0, m == MT - 1)
                last.then_inc(h_full.sem, 1)

            def fc2(b, g, first):
                wait(pe, h_lo_r, b, g + 1)
                if g == 0 and first:
                    pe.wait_ge(w2_lo_r, 1)
                elif g == 0:
                    wait(pe, changed, b - 1, MT)
                for m in range(MT):
                    ms = slice(m * P, m * P + P)
                    last = split3(nc, obank[:, m, :], w2_hi[:, g, ms], w2_lo[:, g, ms],
                                  h_hi[:, g % 4, :], h_lo[:, g % 4, :], g == 0, g == G - 1)
                last.then_inc(h_used.sem, 1)

            def body(b, par, last, first):
                more = not (last and par)
                wait(pe, ll_lo_r, b, 1)
                for g in range(G):
                    if more and g in MEAN_PE:
                        norm.pe_mean(pe, b + 1, MEAN_PE.index(g))
                    if more and g == VAR_PE[0]:
                        wait(pe, meaned, b + 1, 2)
                        norm.pe_var(pe, b + 1, 0)
                    fc1(b, g)
                    if more and g == VAR_PE[1]:
                        norm.pe_var(pe, b + 1, 1)
                    if g >= LAG:
                        fc2(b, g - LAG, first)
                for g in range(G - LAG, G):
                    fc2(b, g, first)

            batches(pe, body)


def program(nc, x, wqkv_t, wproj_t, bproj, fc1_t, fc1_b, interp, fc2_t, fc2_b, scratch, out):
    by_batch = "b (p j) n -> b p j n"
    x1 = scratch.rearrange(by_batch, j=J)
    with (
        nc.sbuf_tensor("tokens", [P, 2, J, N], F32) as two,
        nc.sbuf_tensor("centred", [P, J, N], F32) as one,
        nc.sbuf_tensor("spare", [P, N], F32) as spare,
        nc.semaphore("handed") as handed,
        nc.semaphore("x1_stored") as x1_stored,
    ):
        x1_stored = Count(x1_stored, 32)
        attention(nc, two, one, spare, handed, x1_stored, x.rearrange(by_batch, j=J), wqkv_t, wproj_t, bproj,
                  x1, fc1_t, interp)
        feed_forward(nc, two, one, spare, handed, x1_stored, x1, fc1_t, fc1_b, fc2_t, fc2_b,
                     out.rearrange(by_batch, j=J))


def kernel(**inputs):
    import numpy as np
    import concourse.bacc as bacc
    from concourse.bass_utils import run_bass_kernel_spmd

    a = {k: np.ascontiguousarray(v) for k, v in inputs.items()}
    pos = np.arange(C, dtype=np.float32) / np.float32(C - 1) * np.float32(M2 - 1)
    at = np.clip(np.floor(pos).astype(np.int32), 0, M2 - 2)
    frac = (pos - at.astype(np.float32)).astype(np.float32)
    interp = np.zeros((C, M2), np.float32)
    interp[np.arange(C), at] = np.float32(1.0) - frac
    interp[np.arange(C), at + 1] = frac

    def tiles(w):
        return np.ascontiguousarray(w.reshape(-1, P, w.shape[1]).transpose(1, 0, 2))

    def by_tile(w, j):
        return np.ascontiguousarray(w.reshape(w.shape[0], P, j).transpose(0, 2, 1).reshape(w.shape[0], -1))

    arrays = {
        "x": a["x"].reshape(B, C, N),
        "wqkv_t": np.ascontiguousarray(a["L0_conv_w_qkv"].T).reshape(P, J, 3 * C),
        "wproj_t": tiles(by_tile(np.ascontiguousarray(a["L0_conv_w_proj"].T), J)),
        "bproj": a["L0_conv_b_proj"].reshape(P, J),
        "fc1_t": tiles(np.ascontiguousarray(a["L0_ffn_fc1_w"].T)),
        "fc1_b": np.ascontiguousarray(a["L0_ffn_fc1_b"].reshape(G, P).T),
        "interp": tiles(by_tile(interp, MT)),
        "fc2_t": tiles(by_tile(np.ascontiguousarray(a["L0_ffn_fc2_w"].T), MT)),
        "fc2_b": a["L0_ffn_fc2_b"].reshape(P, MT),
    }
    nc = bacc.Bacc("TRN2", target_bir_lowering=False, num_devices=1)
    aps = [nc.dram_tensor(f"in_{k}", v.shape, F32, kind="ExternalInput").ap() for k, v in arrays.items()]
    scratch = nc.dram_tensor("x1_scratch", (B, C, N), F32, kind="Internal").ap()
    out = nc.dram_tensor("out_0_dram", (B, C, N), F32, kind="ExternalOutput").ap()
    program(nc, *aps, scratch, out)
    r = run_bass_kernel_spmd(nc, [{f"in_{k}": v for k, v in arrays.items()}], core_ids=[0])
    return r.results[0]["out_0_dram"].reshape(B, C, 32, 32)
```
